# Optimizing a Trainium2 kernel written in Bass

```python
import numpy as np
import jax
import jax.numpy as jnp

def _softmax(x, axis=-1):
    return jax.nn.softmax(x, axis=axis)

def _gelu(x):
    return jax.nn.gelu(x, approximate=True)

def _silu(x):
    return jax.nn.silu(x)

def _sigmoid(x):
    return jax.nn.sigmoid(x)

def _layernorm(x, axis=-1, eps=1e-05):
    m = jnp.mean(x, axis=axis, keepdims=True)
    v = jnp.var(x, axis=axis, keepdims=True)
    return (x - m) / jnp.sqrt(v + eps)

def _scatter_add(tgt, idx, src, axis=0):
    return tgt.at[idx].add(src)

def _segment_sum(src, seg, n):
    return jax.ops.segment_sum(src, seg, n)
kernel_name = 'mk_gnn_resnorm_d1_gnn_r8_7c8440'

def setup_inputs(seed: int=0):
    np.random.seed(seed)
    _w = jnp.asarray

    def _rec_inputs():
        import jax
        import jax.numpy as jnp
        _gk = jax.random.key(seed)
        x = -0.0006008 + 1.001 * jax.random.normal(jax.random.fold_in(_gk, 1), (6250, 128), jnp.float32)
        src = jax.random.randint(jax.random.fold_in(_gk, 2), (200000,), 0, 6250, jnp.int32)
        dst = jax.random.randint(jax.random.fold_in(_gk, 3), (200000,), 0, 6250, jnp.int32)
        _o = jnp.argsort(dst, stable=True)
        src = src[_o]
        dst = dst[_o]
        edge_attr_256 = -8.48674e-05 + 0.999927 * jax.random.normal(jax.random.fold_in(_gk, 11), (200000, 256), jnp.float32)
        return (x, src, dst, edge_attr_256)
    x, src, dst, edge_attr_256 = _rec_inputs()

    def _L0_gnn_setup():
        import jax, jax.numpy as jnp
        import numpy as np
        N_NODES = 2500
        N_EDGES = 80000
        H = 128
        IN = 128
        SCALE = 30.0
        EPS = 1e-05

        def _layernorm(x, g, b):
            mu = jnp.mean(x, axis=-1, keepdims=True)
            var = jnp.mean(jnp.square(x - mu), axis=-1, keepdims=True)
            return (x - mu) * jax.lax.rsqrt(var + EPS) * g + b
        key = jax.random.key(seed)
        ks = jax.random.split(key, 10)
        s = 0.05
        return {'h_V': jax.random.normal(ks[0], (N_NODES, H), jnp.float32), 'h_E': jax.random.normal(ks[1], (N_EDGES, H + IN), jnp.float32), 'edge_idx': jax.random.randint(ks[2], (2, N_EDGES), 0, N_NODES, jnp.int64), 'W1_w': jax.random.normal(ks[3], (H, H + IN), jnp.float32) * s, 'W1_b': jnp.zeros((H,), jnp.float32), 'W2_w': jax.random.normal(ks[4], (H, H), jnp.float32) * s, 'W2_b': jnp.zeros((H,), jnp.float32), 'W3_w': jax.random.normal(ks[5], (H, H), jnp.float32) * s, 'W3_b': jnp.zeros((H,), jnp.float32), 'ln1_g': jnp.ones((H,), jnp.float32), 'ln1_b': jnp.zeros((H,), jnp.float32), 'd1_w': jax.random.normal(ks[6], (4 * H, H), jnp.float32) * s, 'd1_b': jnp.zeros((4 * H,), jnp.float32), 'd2_w': jax.random.normal(ks[7], (H, 4 * H), jnp.float32) * s, 'd2_b': jnp.zeros((H,), jnp.float32), 'ln2_g': jnp.ones((H,), jnp.float32), 'ln2_b': jnp.zeros((H,), jnp.float32)}
    _L0_gnn_all = _L0_gnn_setup()
    _L0_gnn_in = {k: v for k, v in _L0_gnn_all.items() if k in ('W1_w', 'W1_b', 'W2_w', 'W2_b', 'W3_w', 'W3_b', 'ln1_g', 'ln1_b', 'd1_w', 'd1_b', 'd2_w', 'd2_b', 'ln2_g', 'ln2_b')}
    del _L0_gnn_all
    return {'x': x, 'src': src, 'dst': dst, 'edge_attr_256': edge_attr_256, 'L0_gnn_W1_w': _L0_gnn_in['W1_w'], 'L0_gnn_W1_b': _L0_gnn_in['W1_b'], 'L0_gnn_W2_w': _L0_gnn_in['W2_w'], 'L0_gnn_W2_b': _L0_gnn_in['W2_b'], 'L0_gnn_W3_w': _L0_gnn_in['W3_w'], 'L0_gnn_W3_b': _L0_gnn_in['W3_b'], 'L0_gnn_ln1_g': _L0_gnn_in['ln1_g'], 'L0_gnn_ln1_b': _L0_gnn_in['ln1_b'], 'L0_gnn_d1_w': _L0_gnn_in['d1_w'], 'L0_gnn_d1_b': _L0_gnn_in['d1_b'], 'L0_gnn_d2_w': _L0_gnn_in['d2_w'], 'L0_gnn_d2_b': _L0_gnn_in['d2_b'], 'L0_gnn_ln2_g': _L0_gnn_in['ln2_g'], 'L0_gnn_ln2_b': _L0_gnn_in['ln2_b']}

def reference(x, src, dst, edge_attr_256, L0_gnn_W1_w, L0_gnn_W1_b, L0_gnn_W2_w, L0_gnn_W2_b, L0_gnn_W3_w, L0_gnn_W3_b, L0_gnn_ln1_g, L0_gnn_ln1_b, L0_gnn_d1_w, L0_gnn_d1_b, L0_gnn_d2_w, L0_gnn_d2_b, L0_gnn_ln2_g, L0_gnn_ln2_b):
    import jax
    import jax.numpy as jnp

    def _L0_gnn_ref(h_V, h_E, edge_idx, W1_w, W1_b, W2_w, W2_b, W3_w, W3_b, ln1_g, ln1_b, d1_w, d1_b, d2_w, d2_b, ln2_g, ln2_b):
        import jax, jax.numpy as jnp
        import numpy as np
        N_NODES = 2500
        N_EDGES = 80000
        H = 128
        IN = 128
        SCALE = 30.0
        EPS = 1e-05

        def _layernorm(x, g, b):
            mu = jnp.mean(x, axis=-1, keepdims=True)
            var = jnp.mean(jnp.square(x - mu), axis=-1, keepdims=True)
            return (x - mu) * jax.lax.rsqrt(var + EPS) * g + b
        src_idx = edge_idx[0]
        m = jax.nn.relu(h_E @ W1_w.T + W1_b)
        m = jax.nn.relu(m @ W2_w.T + W2_b)
        m = m @ W3_w.T + W3_b
        dh = jax.ops.segment_sum(m, src_idx, num_segments=h_V.shape[0]) / SCALE
        h = _layernorm(h_V + dh, ln1_g, ln1_b)
        dh2 = jax.nn.relu(h @ d1_w.T + d1_b) @ d2_w.T + d2_b
        return _layernorm(h + dh2, ln2_g, ln2_b)
    edge_index = jnp.stack([src, dst])
    x = _layernorm(x + _L0_gnn_ref(x, edge_attr_256, edge_index, L0_gnn_W1_w, L0_gnn_W1_b, L0_gnn_W2_w, L0_gnn_W2_b, L0_gnn_W3_w, L0_gnn_W3_b, L0_gnn_ln1_g, L0_gnn_ln1_b, L0_gnn_d1_w, L0_gnn_d1_b, L0_gnn_d2_w, L0_gnn_d2_b, L0_gnn_ln2_g, L0_gnn_ln2_b), axis=-1)
    return x

_drawn_inputs = setup_inputs


def setup_inputs(seed=0):
    import zlib

    import numpy as np

    out = dict(_drawn_inputs(seed))
    spreads = {'L0_gnn_W1_b': (0.0, 2.0),
     'L0_gnn_W2_b': (0.0, 1.101),
     'L0_gnn_W3_b': (0.0, 0.377),
     'L0_gnn_ln1_g': (1.0, 0.2),
     'L0_gnn_ln1_b': (0.0, 0.1),
     'L0_gnn_d1_b': (0.0, 0.1),
     'L0_gnn_d2_b': (0.0, 0.1),
     'L0_gnn_ln2_g': (1.0, 0.2),
     'L0_gnn_ln2_b': (0.0, 0.1)}
    factors = {'edge_attr_256': 6.011, 'L0_gnn_W1_w': 5.951}
    for name, (base, spread) in spreads.items():
        noise = np.random.default_rng([zlib.crc32(name.encode()), seed]).standard_normal(out[name].shape)
        drawn = base * np.exp(spread * noise) if base else spread * noise
        out[name] = jnp.asarray(drawn.astype(out[name].dtype))
    for name, factor in factors.items():
        out[name] = (out[name] * factor).astype(out[name].dtype)
    return out
```

```python
from contextlib import ExitStack

import concourse.bass as bass
from concourse import mybir

ALU = mybir.AluOpType
ACT = mybir.ActivationFunctionType
F32 = mybir.dt.float32
BF16 = mybir.dt.bfloat16
I32 = mybir.dt.int32

P = 128
H = 128
K_IN = 256
KC = K_IN // P
FF = 512
FC = FF // P
NODES = 6250
EDGES = 200000
SCALE = 30.0
EPS = 1e-5

TPB = 4
BLOCK = TPB * P
UNROLL = 4
BLOCKS = -(-EDGES // (BLOCK * UNROLL)) * UNROLL
PADDED_EDGES = BLOCKS * BLOCK

GROUPS = -(-NODES // (TPB * P))
CPP = GROUPS * TPB
PADDED_NODES = P * CPP
TRASH = PADDED_NODES
ROWS = PADDED_NODES + P
RPP = ROWS // P
DIV_SHIFT = 14
DIV_MUL = -(-(1 << DIV_SHIFT) // (CPP // 4))
assert CPP % 4 == 0 and all((n // 4 * DIV_MUL) >> DIV_SHIFT == n // CPP for n in range(PADDED_NODES))
assert PADDED_NODES // 4 * DIV_MUL < 1 << 24

TABLE_BLOCKS = 1
TABLES = TABLE_BLOCKS * TPB


class Step:

    def __init__(self, base, n, unroll):
        self.base, self.n, self.unroll = base, n, unroll
        self.slot = n % unroll

    def ahead(self, k):
        return Step(self.base, self.n + k, self.unroll)

    def number(self):
        return self.n if self.base is None else self.base * self.unroll + self.n

    def exists(self, count):
        return self.base is not None or 0 <= self.n < count


def steps(eng, count, unroll, lead):
    for n in range(-lead, 0):
        yield Step(None, n, unroll)
    turns = (count - lead) // unroll
    with eng.Fori(0, turns) as turn:
        for slot in range(unroll):
            yield Step(turn, slot, unroll)
    for n in range(turns * unroll, count):
        yield Step(None, n, unroll)


def after(eng, sems, step, inc=1):
    if step.base is None:
        if step.n >= 0:
            eng.wait_ge(sems[step.slot], (step.n // step.unroll + 1) * inc)
    else:
        assert step.n >= -step.unroll
        eng.wait_ge(sems[step.slot], (step.base + (step.n // step.unroll + 1)) * inc)


def apart(eng):
    eng.nop(nofuse=True)


def build(nc, edges_t, src_cols, x, w1t, w2t, w3t, b1, b2, b3, g1, be1, d1t, d1b, d2t, d2b, g2, be2, out):
    with ExitStack() as ctx:
        def sb(name, shape, dt=F32):
            return ctx.enter_context(nc.sbuf_tensor(name, shape, dt))

        def ps(name, shape):
            return ctx.enter_context(nc.psum_tensor(name, shape, F32))

        def sem(name):
            return ctx.enter_context(nc.semaphore(name))

        def sems(name, n):
            return [sem(f"{name}{k}") for k in range(n)]

        tables = [nc.dram_tensor(f"node_sums{t}", (ROWS, H), F32, kind="Internal").ap() for t in range(TABLES)]

        rows_ps = ps("rows_ps", [P, TPB, P])
        h1_ps = [ps(f"h1_ps{k}", [P, BLOCK]) for k in range(2)]
        h2_ps = [ps(f"h2_ps{k}", [P, TPB, H]) for k in range(2)]
        sum_ps = [ps(f"sum_ps{k}", [P, TPB, H]) for k in range(2)]
        count_ps = ps("count_ps", [P, CPP])

        ident = sb("ident", [P, P])
        not_before = sb("not_before", [P, P])
        iota_i = sb("iota_i", [P, P], I32)
        iota = sb("iota", [P, P], BF16)
        trash_i = sb("trash_i", [P, 1], I32)
        trash = sb("trash", [P, 1])
        ones3 = sb("ones3", [3, P], BF16)
        zero_h = sb("zero_h", [P, P], BF16)
        zeros_then_x = sb("zeros_then_x", [P, RPP * H])
        x_sb = zeros_then_x[:, 0:CPP * H].rearrange("p (c f) -> p c f", f=H)
        w1_sb = sb("w1_sb", [P, KC, H])
        w2_sb = sb("w2_sb", [P, H])
        w3_sb = sb("w3_sb", [P, H])
        d1_sb = sb("d1_sb", [P, FF])
        d2_sb = sb("d2_sb", [P, FC, H])
        b1_sb = sb("b1_sb", [P, 1])
        d1b_sb = sb("d1b_sb", [P, FC])
        b2_row = sb("b2_row", [3, H])
        b2_rest = sb("b2_rest", [3, 2, H])
        b2_part = sb("b2_part", [3, 3, H], BF16)
        b2_sum = sb("b2_sum", [3, 2, H])
        b2_split = sb("b2_split", [3, H], BF16)
        bcast = sb("bcast", [P, 6, H])
        B3, G1, BE1, D2B, G2, BE2 = (bcast[:, k, :] for k in range(6))

        src_sb = sb("src_sb", [P, BLOCKS, TPB], I32)
        div_sb = sb("div_sb", [P, BLOCKS, TPB], I32)
        ids = sb("ids", [P, BLOCKS, 3, TPB])

        edge_in = [sb(f"edge_in{k}", [P, KC, BLOCK]) for k in range(UNROLL)]
        ids_now = [sb(f"ids_now{k}", [P, 3, TPB]) for k in range(UNROLL)]
        same = [sb(f"same{k}", [P, TPB, P]) for k in range(UNROLL)]
        rank = [sb(f"rank{k}", [P, TPB]) for k in range(UNROLL)]
        dest_f = [sb(f"dest_f{k}", [P, TPB]) for k in range(UNROLL)]
        dest = [sb(f"dest{k}", [P, TPB], I32) for k in range(UNROLL)]
        hot_p = [sb(f"hot_p{k}", [P, TPB, P], BF16) for k in range(UNROLL)]
        hot_c = [sb(f"hot_c{k}", [P, TPB, CPP], BF16) for k in range(UNROLL)]
        h1 = [sb(f"h1_{k}", [P, BLOCK]) for k in range(2)]
        h2 = [sb(f"h2_{k}", [P, TPB, H]) for k in range(2)]
        sums = [sb(f"sums{k}", [P, TPB, H]) for k in range(UNROLL)]

        tab_in = [sb(f"tab_in{k}", [P, TABLES, TPB, H]) for k in range(2)]
        pair_sum = sb("pair_sum", [P, TABLES // 2, TPB, H])
        agg = [sb(f"agg{k}", [P, TPB, H]) for k in range(2)]
        agg_t = [sb(f"agg_t{k}", [P, BLOCK]) for k in range(2)]
        count_sb = sb("count_sb", [P, CPP])
        bias = sb("bias", [P, TPB, H])
        resid = [sb(f"resid{k}", [P, TPB, H]) for k in range(2)]
        y = sb("y", [P, TPB, H])
        normed = sb("normed", [P, TPB, H])
        scaled = sb("scaled", [P, TPB, H])
        hn = [sb(f"hn{k}", [P, TPB, H]) for k in range(2)]
        hb = [sb(f"hb{k}", [P, TPB, H]) for k in range(2)]
        hn_t = [sb(f"hn_t{k}", [P, BLOCK]) for k in range(2)]
        hid = [sb(f"hid{k}", [P, FC, BLOCK]) for k in range(2)]
        xb = [sb(f"xb{k}", [P, TPB, H]) for k in range(2)]
        out_sb = [sb(f"out_sb{k}", [P, TPB, H]) for k in range(2)]
        stats = sb("stats", [P, TPB, 6])
        mean_var = sb("mean_var", [P, TPB, 2])
        std = sb("std", [P, TPB])
        rstd = sb("rstd", [P, TPB])
        eps = sb("eps", [P, 1])

        weights_in = sem("weights_in")
        src_in = sem("src_in")
        consts_made = sem("consts_made")
        dve_step = sem("dve_step")
        zeros_made = sem("zeros_made")
        eps_made = sem("eps_made")
        pool_step = sem("pool_step")
        tables_zeroed = sems("tables_zeroed", TABLES)
        pe_const = sem("pe_const")
        edges_in = sems("edges_in", UNROLL)
        ids_ready = sems("ids_ready", UNROLL)
        rows_ready = sems("rows_ready", UNROLL)
        h1_done = sems("h1_done", UNROLL)
        h1_ready = sems("h1_ready", UNROLL)
        h2_done = sems("h2_done", UNROLL)
        h2_ready = sems("h2_ready", UNROLL)
        rank_made = sems("rank_made", UNROLL)
        dest_f_made = sems("dest_f_made", UNROLL)
        dest_ready = sems("dest_ready", UNROLL)
        hot_ready = sems("hot_ready", UNROLL)
        sum_done = sems("sum_done", UNROLL)
        sums_ready = sems("sums_ready", UNROLL)
        scattered = [sems(f"scattered{t}_", UNROLL) for t in range(TPB)]
        edges_done = sem("edges_done")
        counts_done = sem("counts_done")
        counts_ready = sem("counts_ready")
        x_all_in = sem("x_all_in")
        tables_in = sems("tables_in", 2)
        agg_step = sems("agg_step", 2)
        agg_ready = sems("agg_ready", 2)
        agg_turned = sems("agg_turned", 2)
        agg_t_ready = sems("agg_t_ready", 2)
        bias_made = sems("bias_made", 2)
        resid_ready = sems("resid_ready", 2)
        dh_done = sems("dh_done", 2)
        norm_step = sems("norm_step", 2)
        var_ready = [sems(f"var_ready{k}_", 2) for k in range(3)]
        std_ready = [sems(f"std_ready{k}_", 2) for k in range(3)]
        hn_ready = sems("hn_ready", 2)
        hb_ready = sems("hb_ready", 2)
        xb_ready = sems("xb_ready", 2)
        hn_turned = sems("hn_turned", 2)
        hn_t_ready = sems("hn_t_ready", 2)
        hid_done = [sems(f"hid_done{c}_", 2) for c in range(FC)]
        hid_ready = [sems(f"hid_ready{c}_", 2) for c in range(FC)]
        ff_done = sems("ff_done", 2)
        y1_made = sems("y1_made", 2)
        y2_made = sems("y2_made", 2)
        y3_made = sems("y3_made", 2)
        out_ready = sems("out_ready", 2)
        stored = sems("stored", 2)

        WEIGHTS = 16
        PE_CONSTS = 3

        block = ctx.enter_context(nc.Block())

        @block.sync
        def _(sp):
            sp.dma_start(src_sb[:], src_cols).then_inc(src_in, 16)
            for dst, of in (
                (w1_sb[:], w1t.rearrange("(k p) f -> p k f", p=P)),
                (w2_sb[:], w2t), (w3_sb[:], w3t), (d1_sb[:], d1t),
                (d2_sb[:], d2t.rearrange("(c p) f -> p c f", p=P)),
                (b1_sb[:], b1), (d1b_sb[:], d1b),
                (b2_row[0:1, :], b2), (b2_row[1:2, :], b2), (b2_row[2:3, :], b2),
            ):
                sp.dma_start(dst, of).then_inc(weights_in, 16)
            for k, row in enumerate((b3, g1, be1, d2b, g2, be2)):
                sp.dma_start(bcast[:, k, :], row.to_broadcast([P, H])).then_inc(weights_in, 16)

            def load(s):
                after(sp, h1_done, s.ahead(-UNROLL))
                sp.dma_start(edge_in[s.slot][:], edges_t[s.number()]).then_inc(edges_in[s.slot], 16)

            for n in range(UNROLL):
                load(Step(None, n, UNROLL))
            sp.wait_ge(zeros_made, 1)
            for t in range(TABLES):
                sp.dma_start(tables[t].rearrange("(p r) f -> p (r f)", p=P),
                             zeros_then_x[:]).then_inc(tables_zeroed[t], 16)
            for t in range(TABLES):
                sp.wait_ge(tables_zeroed[t], 16)
            sp.dma_start(x_sb, x.rearrange("(p c) f -> p c f", p=P)).then_inc(x_all_in, 16)
            with sp.Fori(1, BLOCKS // UNROLL) as turn:
                for k in range(UNROLL):
                    load(Step(turn, k, UNROLL))

            def nodes(ap, g):
                return ap.rearrange("(p g c) f -> g p c f", g=GROUPS, c=TPB)[g]

            def load_tables(s):
                after(sp, agg_ready, s.ahead(-2))
                for t in range(TABLES):
                    sp.dma_start(tab_in[s.slot][:, t], nodes(tables[t][0:PADDED_NODES], s.number())
                                 ).then_inc(tables_in[s.slot], 16)

            def store(s):
                after(sp, out_ready, s)
                sp.dma_start(nodes(out, s.number()), out_sb[s.slot][:]).then_inc(stored[s.slot], 16)

            sp.wait_ge(edges_done, 1)
            for s in steps(sp, GROUPS, 2, 2):
                if s.ahead(2).exists(GROUPS):
                    load_tables(s.ahead(2))
                if s.exists(GROUPS):
                    store(s)
            for q in range(2):
                sp.wait_ge(stored[q], 16 * ((GROUPS + 1 - q) // 2))

        @block.gpsimd
        def _(pool):
            nc.gpsimd.memset(ident[:], 0.0).then_inc(pool_step, 1)
            nc.gpsimd.memset(not_before[:], 1.0).then_inc(pool_step, 1)
            pool.wait_ge(pool_step, 2)
            nc.gpsimd.affine_select(out=ident[:], in_=ident[:], compare_op=ALU.not_equal, fill=1.0, base=0,
                                    pattern=[[-1, P]], channel_multiplier=1).then_inc(consts_made, 1)
            nc.gpsimd.affine_select(out=not_before[:], in_=not_before[:], compare_op=ALU.is_ge, fill=0.0, base=0,
                                    pattern=[[-1, P]], channel_multiplier=1).then_inc(consts_made, 1)
            nc.gpsimd.iota(iota_i[:], [[1, P]], base=0, channel_multiplier=0).then_inc(consts_made, 1)
            nc.gpsimd.iota(trash_i[:], [[0, 1]], base=TRASH, channel_multiplier=1).then_inc(consts_made, 1)

            def scatter(s):
                after(pool, sums_ready, s)
                after(pool, dest_ready, s)
                before = s.ahead(-TABLE_BLOCKS)
                for t in range(TPB):
                    after(pool, scattered[t], before, 16)
                    table = tables[(s.slot % TABLE_BLOCKS) * TPB + t]
                    if s.base is None and s.n < TABLE_BLOCKS:
                        pool.wait_ge(tables_zeroed[s.n * TPB + t], 16)
                    apart(pool)
                    pool.indirect_dma_start(
                        table, bass.IndirectOffsetOnAxis(ap=dest[s.slot][:, t:t + 1], axis=0),
                        sums[s.slot][:, t, :], None, compute_op=ALU.add).then_inc(scattered[t][s.slot], 16)

            for n in range(UNROLL):
                scatter(Step(None, n, UNROLL))
            with pool.Fori(1, BLOCKS // UNROLL) as turn:
                for k in range(UNROLL):
                    scatter(Step(turn, k, UNROLL))
            for t in range(TPB):
                for k in range(UNROLL):
                    pool.wait_ge(scattered[t][k], 16 * (BLOCKS // UNROLL))
            pool.sem_inc(edges_done, 1)

            def add_tables(s):
                q = s.slot
                after(pool, tables_in, s, 16 * TABLES)
                after(pool, agg_turned, s.ahead(-2))
                after(pool, agg_ready, s.ahead(-1))
                for k in range(TABLES // 2):
                    nc.gpsimd.tensor_tensor(pair_sum[:, k], tab_in[q][:, 2 * k], tab_in[q][:, 2 * k + 1],
                                            ALU.add).then_inc(agg_step[q], 1)
                after(pool, agg_step, s, TABLES // 2)
                nc.gpsimd.tensor_tensor(agg[q][:], pair_sum[:, 0], pair_sum[:, 1], ALU.add).then_inc(agg_ready[q], 1)

            def residuals(s):
                q, c = s.slot, s.number() * TPB
                after(pool, y1_made, s.ahead(-2))
                after(pool, resid_ready, s.ahead(-1))
                apart(pool)
                nc.gpsimd.tensor_tensor(bias[:], B3.unsqueeze(1).to_broadcast([P, TPB, H]),
                                        count_sb[:, bass.ds(c, TPB)].unsqueeze(2).to_broadcast([P, TPB, H]),
                                        ALU.mult).then_inc(bias_made[q], 1)
                after(pool, bias_made, s)
                apart(pool)
                nc.gpsimd.tensor_tensor(resid[q][:], bias[:], x_sb[:, bass.ds(c, TPB), :], ALU.add).then_inc(resid_ready[q], 1)
                after(pool, out_ready, s.ahead(-2))
                apart(pool)
                nc.gpsimd.tensor_tensor(xb[q][:], BE2.unsqueeze(1).to_broadcast([P, TPB, H]),
                                        x_sb[:, bass.ds(c, TPB), :], ALU.add).then_inc(xb_ready[q], 1)

            def add_d2b(s):
                q = s.slot
                after(pool, hn_ready, s)
                after(pool, y2_made, s.ahead(-2))
                nc.gpsimd.tensor_tensor(hb[q][:], hn[q][:], D2B.unsqueeze(1).to_broadcast([P, TPB, H]),
                                        ALU.add).then_inc(hb_ready[q], 1)

            pool.wait_ge(counts_ready, 1)
            pool.wait_ge(x_all_in, 16)
            pool.wait_ge(weights_in, 16 * WEIGHTS)
            for s in steps(pool, GROUPS, 2, 2):
                if s.ahead(2).exists(GROUPS):
                    add_tables(s.ahead(2))
                if s.ahead(1).exists(GROUPS):
                    residuals(s.ahead(1))
                if s.exists(GROUPS):
                    add_d2b(s)

        @block.scalar
        def _(act):
            def relu1(s):
                after(act, h1_done, s)
                after(act, h2_done, s.ahead(-2))
                nc.scalar.activation(h1[s.slot % 2][:], h1_ps[s.slot % 2][:], ACT.Relu,
                                     bias=b1_sb[:, 0:1]).then_inc(h1_ready[s.slot], 1)

            def relu2(s):
                after(act, h2_done, s)
                after(act, sum_done, s.ahead(-2))
                nc.scalar.activation(h2[s.slot % 2][:], h2_ps[s.slot % 2][:], ACT.Relu).then_inc(h2_ready[s.slot], 1)

            def take_sums(s):
                after(act, sum_done, s)
                for t in range(TPB):
                    after(act, scattered[t], s.ahead(-UNROLL), 16)
                nc.scalar.copy(sums[s.slot][:], sum_ps[s.slot % 2][:]).then_inc(sums_ready[s.slot], 1)

            act.wait_ge(weights_in, 16 * WEIGHTS)
            for s in steps(act, BLOCKS, UNROLL, 2):
                if s.ahead(2).exists(BLOCKS):
                    relu1(s.ahead(2))
                if s.ahead(1).exists(BLOCKS):
                    relu2(s.ahead(1))
                if s.exists(BLOCKS):
                    take_sums(s)

            act.wait_ge(counts_done, 1)
            nc.scalar.mul(count_sb[:], count_ps[:], 1.0 / SCALE).then_inc(counts_ready, 1)

            def take_agg(s):
                after(act, agg_turned, s)
                after(act, dh_done, s.ahead(-2))
                nc.scalar.copy(agg_t[s.slot][:], rows_ps[:].rearrange("p t n -> p (t n)")).then_inc(agg_t_ready[s.slot], 1)

            def take_hn(s):
                after(act, hn_turned, s)
                after(act, hid_done[FC - 1], s.ahead(-2))
                nc.scalar.copy(hn_t[s.slot][:], sum_ps[0][:].rearrange("p t n -> p (t n)")).then_inc(hn_t_ready[s.slot], 1)

            def take_hidden(s, c):
                after(act, hid_done[c], s)
                after(act, ff_done, s.ahead(-2))
                nc.scalar.activation(hid[s.slot][:, c, :], h1_ps[c % 2][:], ACT.Relu,
                                     bias=d1b_sb[:, c:c + 1]).then_inc(hid_ready[c][s.slot], 1)

            def root(s, k):
                after(act, var_ready[k], s)
                nc.scalar.activation(std[:], mean_var[:, :, 1], ACT.Sqrt, bias=eps[:, 0:1]).then_inc(std_ready[k][s.slot], 1)

            act.wait_ge(eps_made, 1)
            for s in steps(act, GROUPS, 2, 2):
                if s.ahead(2).exists(GROUPS):
                    take_agg(s.ahead(2))
                if s.exists(GROUPS):
                    take_hn(s)
                if s.ahead(1).exists(GROUPS):
                    root(s.ahead(1), 0)
                if s.exists(GROUPS):
                    for c in range(FC):
                        take_hidden(s, c)
                    root(s, 1)
                    root(s, 2)

        @block.tensor
        def _(pe):
            pe.wait_ge(consts_made, 4)
            pe.wait_ge(weights_in, 16 * WEIGHTS)
            pe.wait_ge(pe_const, PE_CONSTS)
            nc.tensor.matmul(count_ps[:], zero_h[:], zero_h[:, 0:CPP], start=True, stop=False)

            def spread_ids(s):
                after(pe, ids_ready, s)
                after(pe, rank_made, s.ahead(-1))
                for t in range(TPB):
                    mm = nc.tensor.transpose(rows_ps[:, t, :], ids_now[s.slot][:, 0, t:t + 1].to_broadcast([P, P]), ident[:])
                mm.then_inc(rows_ready[s.slot], 1)

            def layer1(s):
                after(pe, edges_in, s, 16)
                after(pe, h1_ready, s.ahead(-2))
                for k in range(KC):
                    mm = nc.tensor.matmul(h1_ps[s.slot % 2][:], w1_sb[:, k, :], edge_in[s.slot][:, k, :],
                                          start=(k == 0), stop=(k == KC - 1))
                mm.then_inc(h1_done[s.slot], 1)

            def layer2(s):
                after(pe, h1_ready, s)
                after(pe, h2_ready, s.ahead(-2))
                h2o = h2_ps[s.slot % 2]
                nc.tensor.matmul(h2o[:], ones3[:], b2_split[:].unsqueeze(1).to_broadcast([3, TPB, H]),
                                 start=True, stop=False)
                for t in range(TPB):
                    mm = nc.tensor.matmul(h2o[:, t, :], h1[s.slot % 2][:, t * P:(t + 1) * P], w2_sb[:],
                                          start=False, stop=(t == TPB - 1))
                mm.then_inc(h2_done[s.slot], 1)

            def sum_same(s):
                after(pe, rank_made, s)
                after(pe, h2_ready, s)
                after(pe, sums_ready, s.ahead(-2))
                for t in range(TPB):
                    nc.tensor.matmul(sum_ps[s.slot % 2][:, t, :], same[s.slot][:, t, :], h2[s.slot % 2][:, t, :],
                                     start=True, stop=True)
                after(pe, hot_ready, s)
                for t in range(TPB):
                    mm = nc.tensor.matmul(count_ps[:], hot_p[s.slot][:, t, :], hot_c[s.slot][:, t, :],
                                          start=False, stop=False)
                mm.then_inc(sum_done[s.slot], 1)

            for s in steps(pe, BLOCKS, UNROLL, 2):
                if s.ahead(2).exists(BLOCKS):
                    spread_ids(s.ahead(2))
                    layer1(s.ahead(2))
                if s.ahead(1).exists(BLOCKS):
                    layer2(s.ahead(1))
                if s.exists(BLOCKS):
                    sum_same(s)
            nc.tensor.matmul(count_ps[:], zero_h[:], zero_h[:, 0:CPP], start=False, stop=True).then_inc(counts_done, 1)

            last = Step(None, BLOCKS - 1, UNROLL)
            after(pe, rank_made, last)
            after(pe, h2_ready, last)
            after(pe, sums_ready, last)
            after(pe, sums_ready, last.ahead(-1))

            def turn_agg(s):
                after(pe, agg_ready, s)
                after(pe, agg_t_ready, s.ahead(-1))
                for t in range(TPB):
                    mm = nc.tensor.transpose(rows_ps[:, t, :], agg[s.slot][:, t, :], ident[:])
                mm.then_inc(agg_turned[s.slot], 1)

            def layer3(s):
                after(pe, agg_t_ready, s)
                after(pe, y1_made, s.ahead(-1))
                for t in range(TPB):
                    mm = nc.tensor.matmul(h2_ps[0][:, t, :], agg_t[s.slot][:, t * P:(t + 1) * P], w3_sb[:],
                                          start=True, stop=True)
                mm.then_inc(dh_done[s.slot], 1)

            def turn_hn(s):
                after(pe, hn_ready, s)
                after(pe, hn_t_ready, s.ahead(-1))
                for t in range(TPB):
                    mm = nc.tensor.transpose(sum_ps[0][:, t, :], hn[s.slot][:, t, :], ident[:])
                mm.then_inc(hn_turned[s.slot], 1)

            def hidden(s):
                after(pe, hn_t_ready, s)
                for c in range(FC):
                    if c < 2:
                        after(pe, hid_ready[c + 2], s.ahead(-1))
                    else:
                        after(pe, hid_ready[c - 2], s)
                    nc.tensor.matmul(h1_ps[c % 2][:], d1_sb[:, c * P:(c + 1) * P], hn_t[s.slot][:],
                                     start=True, stop=True).then_inc(hid_done[c][s.slot], 1)

            def project(s):
                after(pe, y2_made, s.ahead(-1))
                for c in range(FC):
                    after(pe, hid_ready[c], s)
                for t in range(TPB):
                    for c in range(FC):
                        mm = nc.tensor.matmul(h2_ps[1][:, t, :], hid[s.slot][:, c, t * P:(t + 1) * P], d2_sb[:, c, :],
                                              start=(c == 0), stop=(c == FC - 1))
                mm.then_inc(ff_done[s.slot], 1)

            for s in steps(pe, GROUPS, 2, 2):
                if s.ahead(2).exists(GROUPS):
                    turn_agg(s.ahead(2))
                if s.ahead(1).exists(GROUPS):
                    layer3(s.ahead(1))
                if s.exists(GROUPS):
                    turn_hn(s)
                    hidden(s)
                    project(s)

        @block.vector
        def _(dve):
            nc.vector.memset(zeros_then_x[:], 0.0).then_inc(zeros_made, 1)
            nc.vector.memset(eps[:], EPS).then_inc(eps_made, 1)
            nc.vector.memset(zero_h[:], 0.0).then_inc(pe_const, 1)
            nc.vector.memset(ones3[:], 1.0).then_inc(pe_const, 1)
            done = [0]

            def then(instruction):
                done[0] += 1
                instruction.then_inc(dve_step, 1)
                dve.wait_ge(dve_step, done[0])

            dve.wait_ge(src_in, 16)
            node, part, col = (ids[:, :, k, :] for k in range(3))
            then(nc.vector.tensor_copy(node, src_sb[:]))
            then(nc.vector.tensor_scalar(div_sb[:], src_sb[:], 2, None, ALU.logical_shift_right))
            then(nc.vector.tensor_scalar(div_sb[:], div_sb[:], DIV_MUL, None, ALU.mult))
            then(nc.vector.tensor_scalar(div_sb[:], div_sb[:], DIV_SHIFT, None, ALU.logical_shift_right))
            then(nc.vector.tensor_copy(part, div_sb[:]))
            then(nc.vector.scalar_tensor_tensor(out=col, in0=part, scalar=-float(CPP), in1=node,
                                                op0=ALU.mult, op1=ALU.add))
            dve.wait_ge(consts_made, 4)
            then(nc.vector.tensor_copy(iota[:], iota_i[:]))
            then(nc.vector.tensor_copy(trash[:], trash_i[:]))
            dve.wait_ge(weights_in, 16 * WEIGHTS)
            then(nc.vector.tensor_copy(b2_part[:, 0], b2_row[:]))
            then(nc.vector.tensor_tensor(b2_rest[:, 0], b2_row[:], b2_part[:, 0], ALU.subtract))
            then(nc.vector.tensor_copy(b2_part[:, 1], b2_rest[:, 0]))
            then(nc.vector.tensor_tensor(b2_rest[:, 1], b2_rest[:, 0], b2_part[:, 1], ALU.subtract))
            then(nc.vector.tensor_copy(b2_part[:, 2], b2_rest[:, 1]))
            then(nc.vector.tensor_scalar(b2_sum[:, 0], b2_part[:, 0], ident[0:3, 0:1], None, ALU.mult))
            then(nc.vector.scalar_tensor_tensor(out=b2_sum[:, 1], in0=b2_part[:, 1], scalar=ident[0:3, 1:2],
                                                in1=b2_sum[:, 0], op0=ALU.mult, op1=ALU.add))
            nc.vector.scalar_tensor_tensor(out=b2_split[:], in0=b2_part[:, 2], scalar=ident[0:3, 2:3],
                                           in1=b2_sum[:, 1], op0=ALU.mult, op1=ALU.add).then_inc(pe_const, 1)

            def take_ids(s):
                after(dve, rows_ready, s.ahead(-UNROLL))
                after(dve, hot_ready, s.ahead(-UNROLL))
                after(dve, dest_ready, s.ahead(-UNROLL))
                nc.vector.tensor_copy(ids_now[s.slot][:], ids[:, s.number()]).then_inc(ids_ready[s.slot], 1)

            def compare(s):
                k = s.slot
                after(dve, rows_ready, s)
                after(dve, ids_ready, s)
                after(dve, sum_done, s.ahead(-UNROLL))
                for t in range(TPB):
                    op = nc.vector.scalar_tensor_tensor(
                        out=same[k][:, t, :], in0=rows_ps[:, t, :], scalar=ids_now[k][:, 0, t:t + 1],
                        in1=not_before[:], op0=ALU.is_equal, op1=ALU.mult, accum_out=rank[k][:, t:t + 1])
                op.then_inc(rank_made[k], 1)

            def choose_rows(s):
                k = s.slot
                for t in range(TPB):
                    after(dve, scattered[t], s.ahead(-UNROLL), 16)
                after(dve, rank_made, s)
                nc.vector.tensor_scalar(dest_f[k][:], rank[k][:], 1.5, trash[:, 0:1],
                                        ALU.is_gt, ALU.mult).then_inc(dest_f_made[k], 1)
                after(dve, dest_f_made, s)
                nc.vector.tensor_tensor(dest[k][:], dest_f[k][:], ids_now[k][:, 0, :], ALU.max).then_inc(dest_ready[k], 1)

            def one_hot(s):
                k = s.slot
                for t in range(TPB):
                    nc.vector.tensor_scalar(hot_p[k][:, t, :], iota[:], ids_now[k][:, 1, t:t + 1], None, ALU.is_equal)
                    op = nc.vector.tensor_scalar(hot_c[k][:, t, :], iota[:, 0:CPP], ids_now[k][:, 2, t:t + 1],
                                                 None, ALU.is_equal)
                op.then_inc(hot_ready[k], 1)

            for s in steps(dve, BLOCKS, UNROLL, 3):
                if s.ahead(3).exists(BLOCKS):
                    take_ids(s.ahead(3))
                if s.ahead(2).exists(BLOCKS):
                    compare(s.ahead(2))
                    one_hot(s.ahead(2))
                    choose_rows(s.ahead(2))

            CHAIN = 10
            link = [0]

            def follow(s, instruction):
                link[0] += 1
                instruction.then_inc(norm_step[s.slot], 1)
                wait_chain(s, link[0])

            def wait_chain(s, n):
                if s.base is None:
                    dve.wait_ge(norm_step[s.slot], s.n // 2 * CHAIN + n)
                else:
                    dve.wait_ge(norm_step[s.slot], (s.base + s.n // 2) * CHAIN + n)

            def normalize(s, dst, var_ready, std_ready):
                for t in range(TPB):
                    op = nc.vector.bn_stats(stats[:, t, :], y[:, t, :])
                follow(s, op)
                apart(dve)
                for t in range(TPB):
                    op = nc.vector.bn_aggr(mean_var[:, t, :], stats[:, t, :])
                op.then_inc(var_ready[s.slot], 1)
                after(dve, std_ready, s)
                follow(s, nc.vector.reciprocal(rstd[:], std[:]))
                for t in range(TPB):
                    op = nc.vector.tensor_scalar(dst[:, t, :], y[:, t, :], mean_var[:, t, 0:1], rstd[:, t:t + 1],
                                                 ALU.subtract, ALU.mult)
                return op

            def spread(row):
                return row.unsqueeze(1).to_broadcast([P, TPB, H])

            def first_norm(s):
                q = s.slot
                link[0] = 0
                after(dve, out_ready, s.ahead(-2))
                after(dve, dh_done, s)
                after(dve, resid_ready, s)
                op = nc.vector.scalar_tensor_tensor(out=y[:], in0=h2_ps[0][:], scalar=1.0 / SCALE, in1=resid[q][:],
                                                    op0=ALU.mult, op1=ALU.add)
                op.then_inc(y1_made[q], 1)
                after(dve, y1_made, s)
                follow(s, normalize(s, normed, var_ready[0], std_ready[0]))
                follow(s, nc.vector.tensor_tensor(scaled[:], normed[:], spread(G1), ALU.mult))
                after(dve, hb_ready, s.ahead(-2))
                nc.vector.tensor_tensor(hn[q][:], scaled[:], spread(BE1), ALU.add).then_inc(hn_ready[q], 1)

            def last_norms(s):
                q = s.slot
                link[0] = 4
                if s.ahead(1).exists(GROUPS):
                    after(dve, hn_ready, s.ahead(1))
                else:
                    after(dve, out_ready, s.ahead(-1))
                after(dve, ff_done, s)
                after(dve, hb_ready, s)
                nc.vector.tensor_tensor(y[:], h2_ps[1][:], hb[q][:], ALU.add).then_inc(y2_made[q], 1)
                after(dve, y2_made, s)
                follow(s, normalize(s, normed, var_ready[1], std_ready[1]))
                follow(s, nc.vector.tensor_tensor(scaled[:], normed[:], spread(G2), ALU.mult))
                after(dve, xb_ready, s)
                after(dve, stored, s.ahead(-2), 16)
                y_again = nc.vector.tensor_tensor(y[:], scaled[:], xb[q][:], ALU.add)
                y_again.then_inc(y3_made[q], 1)
                after(dve, y3_made, s)
                normalize(s, out_sb[q], var_ready[2], std_ready[2]).then_inc(out_ready[q], 1)
                assert link[0] == CHAIN

            for s in steps(dve, GROUPS, 2, 1):
                if s.ahead(1).exists(GROUPS):
                    first_norm(s.ahead(1))
                if s.exists(GROUPS):
                    last_norms(s)


def kernel(x, src, dst, edge_attr_256, L0_gnn_W1_w, L0_gnn_W1_b, L0_gnn_W2_w, L0_gnn_W2_b, L0_gnn_W3_w,
           L0_gnn_W3_b, L0_gnn_ln1_g, L0_gnn_ln1_b, L0_gnn_d1_w, L0_gnn_d1_b, L0_gnn_d2_w, L0_gnn_d2_b,
           L0_gnn_ln2_g, L0_gnn_ln2_b):
    import numpy as np
    import concourse.bacc as bacc
    from concourse.bass_utils import run_bass_kernel_spmd

    def turned(a):
        return np.ascontiguousarray(np.asarray(a).T)

    def row(a):
        return np.asarray(a).reshape(1, -1)

    def column(a, n=P):
        return np.ascontiguousarray(np.asarray(a).reshape(-1, n).T)

    edge_pad = PADDED_EDGES - EDGES
    edges = np.pad(np.asarray(edge_attr_256), ((0, edge_pad), (0, 0)))
    edges_t = np.ascontiguousarray(edges.reshape(BLOCKS, BLOCK, KC, P).transpose(0, 3, 2, 1))
    src_cols = column(np.pad(np.asarray(src), (0, edge_pad), constant_values=NODES)).reshape(P, BLOCKS, TPB)

    arrays = {
        "edges_t": edges_t,
        "src_cols": src_cols,
        "x": np.pad(np.asarray(x), ((0, PADDED_NODES - NODES), (0, 0))),
        "w1t": turned(L0_gnn_W1_w), "w2t": turned(L0_gnn_W2_w), "w3t": turned(L0_gnn_W3_w),
        "b1": column(L0_gnn_W1_b), "b2": row(L0_gnn_W2_b), "b3": row(L0_gnn_W3_b),
        "g1": row(L0_gnn_ln1_g), "be1": row(L0_gnn_ln1_b),
        "d1t": turned(L0_gnn_d1_w), "d1b": column(L0_gnn_d1_b),
        "d2t": turned(L0_gnn_d2_w), "d2b": row(L0_gnn_d2_b),
        "g2": row(L0_gnn_ln2_g), "be2": row(L0_gnn_ln2_b),
    }
    nc = bacc.Bacc("TRN2", target_bir_lowering=False, num_devices=1)
    aps = {n: nc.dram_tensor(n, a.shape, mybir.dt.from_np(a.dtype), kind="ExternalInput").ap()
           for n, a in arrays.items()}
    out = nc.dram_tensor("out", (PADDED_NODES, H), F32, kind="ExternalOutput").ap()
    build(nc, out=out, **aps)
    result = run_bass_kernel_spmd(nc, [arrays], core_ids=[0])
    return result.results[0]["out"][:NODES]
```

```python
from contextlib import ExitStack

import concourse.bass as bass
from concourse import mybir

ALU = mybir.AluOpType
ACT = mybir.ActivationFunctionType
F32 = mybir.dt.float32
F32R = mybir.dt.float32r
BF16 = mybir.dt.bfloat16
I32 = mybir.dt.int32

P = 128
H = 128
K_IN = 256
KC = K_IN // P
FF = 512
FC = FF // P
NODES = 6250
EDGES = 200000
SCALE = 30.0
EPS = 1e-5

TPB = 4
BLOCK = TPB * P
UNROLL = 4
BLOCKS = -(-EDGES // BLOCK)
TILES = -(-EDGES // P)
PADDED_EDGES = BLOCKS * BLOCK

GROUPS = -(-NODES // (TPB * P))
CPP = GROUPS * TPB
PADDED_NODES = P * CPP
TRASH = PADDED_NODES
ROWS = PADDED_NODES + P
RPP = ROWS // P
DIV_SHIFT = 14
DIV_MUL = -(-(1 << DIV_SHIFT) // (CPP // 4))
assert CPP % 4 == 0 and all((n // 4 * DIV_MUL) >> DIV_SHIFT == n // CPP for n in range(PADDED_NODES))
assert PADDED_NODES // 4 * DIV_MUL < 1 << 24

FIRST_IDS = 8
TABLE_BLOCKS = 1
TABLES = TABLE_BLOCKS * TPB

NORM3 = 1
NORM2 = 2
PROJECT = 2
FEED = 3
HN = 4
NORM1 = 5
LAYER3 = 6
TURN = 7
TABLES_AHEAD = 8
NORM_LEADS = (NORM1, NORM2, NORM3)

WEIGHT_COLS = {"w1": KC * H, "b1": 1, "w2": H, "w3": H, "d1": FF, "d1b": FC, "d2": FC * H}
ROW_NAMES = ("b3", "g1", "be1", "d2b", "g2", "be2")


class Step:

    def __init__(self, base, n, unroll):
        self.base, self.n, self.unroll = base, n, unroll
        self.slot = n % unroll

    def ahead(self, k):
        return Step(self.base, self.n + k, self.unroll)

    def number(self):
        return self.n if self.base is None else self.base * self.unroll + self.n

    def exists(self, count):
        return self.base is not None or 0 <= self.n < count


def steps(eng, count, unroll, lead):
    for n in range(-lead, 0):
        yield Step(None, n, unroll)
    turns = (count - 1 - lead) // unroll
    with eng.Fori(0, turns) as turn:
        for slot in range(unroll):
            yield Step(turn, slot, unroll)
    for n in range(turns * unroll, count):
        yield Step(None, n, unroll)


def after(eng, sems, step, inc=1, upto=None):
    back = inc - (inc if upto is None else upto)
    if step.base is None:
        if step.n >= 0:
            eng.wait_ge(sems[step.slot], (step.n // step.unroll + 1) * inc - back)
    else:
        assert (step.n // step.unroll + 1) * inc >= back
        eng.wait_ge(sems[step.slot], step.base * inc + ((step.n // step.unroll + 1) * inc - back))


def apart(eng):
    eng.nop(nofuse=True)


def build(nc, edges_t, src_cols, x, weights, rows, b2_in, out):
    with ExitStack() as ctx:
        def sb(name, shape, dt=F32):
            return ctx.enter_context(nc.sbuf_tensor(name, shape, dt))

        def ps(name, shape):
            return ctx.enter_context(nc.psum_tensor(name, shape, F32))

        def sem(name):
            return ctx.enter_context(nc.semaphore(name))

        def sems(name, n):
            return [sem(f"{name}{k}") for k in range(n)]

        tables = [nc.dram_tensor(f"node_sums{t}", (ROWS, H), F32, kind="Internal").ap() for t in range(TABLES)]

        rows_ps = ps("rows_ps", [P, TPB, P])
        h1_ps = [ps(f"h1_ps{k}", [P, BLOCK]) for k in range(2)]
        h2_ps = [ps(f"h2_ps{k}", [P, TPB, H]) for k in range(2)]
        sum_ps = [ps(f"sum_ps{k}", [P, TPB, H]) for k in range(2)]
        count_ps = ps("count_ps", [P, CPP])

        ident = sb("ident", [P, P])
        not_before = sb("not_before", [P, P])
        iota_i = sb("iota_i", [P, P], I32)
        iota = sb("iota", [P, P], BF16)
        trash_i = sb("trash_i", [P, 1], I32)
        trash = sb("trash", [P, 1])
        ones3 = sb("ones3", [3, P], BF16)
        zero_h = sb("zero_h", [P, P], BF16)
        zeros_then_x = sb("zeros_then_x", [P, RPP * H])
        x_sb = zeros_then_x[:, 0:CPP * H].rearrange("p (c f) -> p c f", f=H)
        weights_sb = sb("weights_sb", [P, sum(WEIGHT_COLS.values())])
        at, part = 0, {}
        for name, width in WEIGHT_COLS.items():
            part[name] = weights_sb[:, at:at + width]
            at += width
        w1_sb = part["w1"].rearrange("p (k f) -> p k f", k=KC)
        w2_sb, w3_sb, d1_sb, b1_sb, d1b_sb = (part[name] for name in ("w2", "w3", "d1", "b1", "d1b"))
        d2_sb = part["d2"].rearrange("p (c f) -> p c f", c=FC)
        b2_row = sb("b2_row", [3, H])
        b2_rest = sb("b2_rest", [3, 2, H])
        b2_part = sb("b2_part", [3, 3, H], BF16)
        b2_sum = sb("b2_sum", [3, 2, H])
        b2_split = sb("b2_split", [3, H], BF16)
        bcast = sb("bcast", [P, len(ROW_NAMES), H])
        B3, G1, BE1, D2B, G2, BE2 = (bcast[:, k, :] for k in range(len(ROW_NAMES)))
        be1_d2b = sb("be1_d2b", [P, H])

        src_sb = sb("src_sb", [P, BLOCKS, TPB], I32)
        ids = sb("ids", [P, BLOCKS, 3, TPB])

        edge_in = [sb(f"edge_in{k}", [P, KC, BLOCK]) for k in range(UNROLL)]
        ids_now = [sb(f"ids_now{k}", [P, 3, TPB]) for k in range(UNROLL)]
        same = [sb(f"same{k}", [P, TPB, P], F32R) for k in range(UNROLL)]
        rank = [sb(f"rank{k}", [P, TPB]) for k in range(UNROLL)]
        dest_f = [sb(f"dest_f{k}", [P, TPB]) for k in range(UNROLL)]
        dest = [sb(f"dest{k}", [P, TPB], I32) for k in range(UNROLL)]
        hot_p = [sb(f"hot_p{k}", [P, TPB, P], BF16) for k in range(UNROLL)]
        hot_c = [sb(f"hot_c{k}", [P, TPB, CPP], BF16) for k in range(UNROLL)]
        h1 = [sb(f"h1_{k}", [P, BLOCK]) for k in range(2)]
        h2_hi = [sb(f"h2_hi{k}", [P, TPB, H], F32R) for k in range(2)]
        h2_lo = [sb(f"h2_lo{k}", [P, TPB, H], F32R) for k in range(2)]
        sums = [sb(f"sums{k}", [P, TPB, H]) for k in range(UNROLL)]

        tab_in = [sb(f"tab_in{k}", [P, TABLES, TPB, H]) for k in range(2)]
        pair_sum = sb("pair_sum", [P, TABLES // 2, TPB, H])
        agg, hn, hn_t = sums[0:2], sums[2:4], h1
        agg_t = [sb(f"agg_t{k}", [P, BLOCK]) for k in range(2)]
        count_sb = sb("count_sb", [P, CPP])
        xb = sb("xb", [P, CPP, H])
        dh_x = sb("dh_x", [P, TPB, H])
        count_now = sb("count_now", [P, TPB])
        y = [[sb(f"y{k}_{q}", [P, TPB, H]) for q in range(2)] for k in range(3)]
        scaled1 = [sb(f"scaled1_{k}", [P, TPB, H]) for k in range(2)]
        scaled2 = sb("scaled2", [P, TPB, H])
        hb = [sb(f"hb{k}", [P, TPB, H]) for k in range(2)]
        hid = [[edge_in[2 * k + c // KC][:, c % KC, :] for c in range(FC)] for k in range(2)]
        normed = [[sb(f"normed{k}_{q}", [P, TPB, H]) for q in range(2)] for k in range(3)]
        stats = [sb(f"stats{k}", [P, TPB, 6]) for k in range(3)]
        mean_var = [sb(f"mean_var{k}", [P, 3, TPB, 2]) for k in range(2)]
        std = [sb(f"std{k}", [P, 3, TPB]) for k in range(2)]
        rstd = [sb(f"rstd{k}", [P, 3, TPB]) for k in range(2)]
        shift = [sb(f"shift{k}", [P, 3, TPB]) for k in range(2)]
        eps = sb("eps", [P, 1])

        weights_in = sem("weights_in")
        rows_in = sem("rows_in")
        src_in = sems("src_in", 2)
        consts_made = sem("consts_made")
        dve_step = sem("dve_step")
        zeros_made = sem("zeros_made")
        eps_made = sem("eps_made")
        pool_step = sem("pool_step")
        tables_zeroed = sems("tables_zeroed", TABLES)
        pe_const = sem("pe_const")
        edges_in = sems("edges_in", UNROLL)
        ids_ready = sems("ids_ready", UNROLL)
        rows_ready = sems("rows_ready", UNROLL)
        h1_done = sems("h1_done", UNROLL)
        h1_ready = sems("h1_ready", UNROLL)
        h2_done = sems("h2_done", UNROLL)
        h2_hi_ready = sems("h2_hi_ready", UNROLL)
        h2_ready = sems("h2_ready", UNROLL)
        rank_made = sems("rank_made", UNROLL)
        dest_f_made = sems("dest_f_made", UNROLL)
        rows_chosen = sems("rows_chosen", UNROLL)
        sum_done = sems("sum_done", UNROLL)
        sums_ready = sems("sums_ready", UNROLL)
        scattered = [sems(f"scattered{t}_", UNROLL) for t in range(TPB)]
        edges_done = sem("edges_done")
        counts_done = sem("counts_done")
        counts_ready = sem("counts_ready")
        x_all_in = sem("x_all_in")
        tables_in = sems("tables_in", 2)
        pairs_added = sems("pairs_added", 2)
        agg_ready = sems("agg_ready", 2)
        agg_turned = sems("agg_turned", 2)
        agg_t_ready = sems("agg_t_ready", 2)
        dh_done = sems("dh_done", 2)
        dh_x_made = sems("dh_x_made", 2)
        y_made = [sems(f"y{k}_made", 2) for k in range(3)]
        stats_made = [sems(f"stats_made{k}_", 2) for k in range(3)]
        var_ready = [sems(f"var_ready{k}_", 2) for k in range(3)]
        std_ready = sems("std_ready", 2)
        rstd_made = sems("rstd_made", 2)
        shift_ready = sems("shift_ready", 2)
        normed_ready = [sems(f"normed_ready{k}_", 2) for k in range(3)]
        scaled1_made = sems("scaled1_made", 2)
        scaled2_made = sems("scaled2_made", 2)
        hn_ready = sems("hn_ready", 2)
        hb_ready = sems("hb_ready", 2)
        xb_ready = sem("xb_ready")
        row_made = sem("row_made")
        hn_turned = sems("hn_turned", 2)
        hn_t_ready = sems("hn_t_ready", 2)
        hid_done = sems("hid_done", 2)
        hid_ready = sems("hid_ready", 2)
        ff_done = sems("ff_done", 2)
        stored = sems("stored", 2)

        WEIGHTS = 2
        PE_CONSTS = 3

        block = ctx.enter_context(nc.Block())

        @block.sync
        def _(sp):
            sp.dma_start(src_sb[:, 0:FIRST_IDS], src_cols[:, 0:FIRST_IDS]).then_inc(src_in[0], 16)
            sp.dma_start(weights_sb[:], weights).then_inc(weights_in, 16)
            sp.dma_start(b2_row[:], b2_in.to_broadcast([3, H])).then_inc(weights_in, 16)

            def load(s):
                after(sp, h1_done, s.ahead(-UNROLL))
                sp.dma_start(edge_in[s.slot][:], edges_t[s.number()]).then_inc(edges_in[s.slot], 16)

            for n in range(UNROLL):
                load(Step(None, n, UNROLL))
            sp.dma_start(src_sb[:, FIRST_IDS:], src_cols[:, FIRST_IDS:]).then_inc(src_in[1], 16)
            sp.dma_start(bcast[:], rows.to_broadcast([P, len(ROW_NAMES) * H]).rearrange(
                "p (k f) -> p k f", f=H)).then_inc(rows_in, 16)
            sp.wait_ge(zeros_made, 1)
            for t in range(TABLES):
                sp.dma_start(tables[t].rearrange("(p r) f -> p (r f)", p=P),
                             zeros_then_x[:]).then_inc(tables_zeroed[t], 16)
            for t in range(TABLES):
                sp.wait_ge(tables_zeroed[t], 16)
            sp.dma_start(x_sb, x.rearrange("(p c) f -> p c f", p=P)).then_inc(x_all_in, 16)
            for s in steps(sp, BLOCKS, UNROLL, UNROLL):
                if s.ahead(UNROLL).exists(BLOCKS) and (s.base is not None or s.n >= 0):
                    load(s.ahead(UNROLL))

            def nodes(ap, g):
                return ap.rearrange("(p g c) f -> g p c f", g=GROUPS, c=TPB)[g]

            def load_tables(s):
                after(sp, agg_ready, s.ahead(-2))
                for t in range(TABLES):
                    sp.dma_start(tab_in[s.slot][:, t], nodes(tables[t][0:PADDED_NODES], s.number())
                                 ).then_inc(tables_in[s.slot], 16)

            def store(s):
                after(sp, normed_ready[2], s)
                sp.dma_start(nodes(out, s.number()), normed[2][s.slot][:]).then_inc(stored[s.slot], 16)

            sp.wait_ge(edges_done, 1)
            for s in steps(sp, GROUPS, 2, TABLES_AHEAD + 1):
                if s.ahead(TABLES_AHEAD + 1).exists(GROUPS):
                    load_tables(s.ahead(TABLES_AHEAD + 1))
                if s.exists(GROUPS):
                    store(s)
            for q in range(2):
                sp.wait_ge(stored[q], 16 * ((GROUPS + 1 - q) // 2))

        @block.gpsimd
        def _(pool):
            nc.gpsimd.memset(ident[:], 0.0).then_inc(pool_step, 1)
            nc.gpsimd.memset(not_before[:], 1.0).then_inc(pool_step, 1)
            pool.wait_ge(pool_step, 2)
            nc.gpsimd.affine_select(out=ident[:], in_=ident[:], compare_op=ALU.not_equal, fill=1.0, base=0,
                                    pattern=[[-1, P]], channel_multiplier=1).then_inc(consts_made, 1)
            nc.gpsimd.affine_select(out=not_before[:], in_=not_before[:], compare_op=ALU.is_ge, fill=0.0, base=0,
                                    pattern=[[-1, P]], channel_multiplier=1).then_inc(consts_made, 1)
            nc.gpsimd.memset(zeros_then_x[:], 0.0).then_inc(zeros_made, 1)
            nc.gpsimd.iota(iota_i[:], [[1, P]], base=0, channel_multiplier=0).then_inc(consts_made, 1)
            nc.gpsimd.iota(trash_i[:], [[0, 1]], base=TRASH, channel_multiplier=1).then_inc(consts_made, 1)

            def scatter(s):
                after(pool, sums_ready, s)
                after(pool, rows_chosen, s)
                before = s.ahead(-TABLE_BLOCKS)
                for t in range(TPB if s.base is not None else min(TPB, TILES - s.n * TPB)):
                    after(pool, scattered[t], before, 16)
                    table = tables[(s.slot % TABLE_BLOCKS) * TPB + t]
                    if s.base is None and s.n < TABLE_BLOCKS:
                        pool.wait_ge(tables_zeroed[s.n * TPB + t], 16)
                    apart(pool)
                    pool.indirect_dma_start(
                        table, bass.IndirectOffsetOnAxis(ap=dest[s.slot][:, t:t + 1], axis=0),
                        sums[s.slot][:, t, :], None, compute_op=ALU.add).then_inc(scattered[t][s.slot], 16)

            for s in steps(pool, BLOCKS, UNROLL, UNROLL):
                if s.ahead(UNROLL).exists(BLOCKS):
                    scatter(s.ahead(UNROLL))
            for t in range(TPB):
                for k in range(UNROLL):
                    pool.wait_ge(scattered[t][k], 16 * len(range(k * TPB + t, TILES, UNROLL * TPB)))
            pool.sem_inc(edges_done, 1)

            def add_tables(s):
                q = s.slot
                after(pool, tables_in, s, 16 * TABLES)
                after(pool, agg_turned, s.ahead(-2))
                after(pool, agg_ready, s.ahead(-1))
                for k in range(TABLES // 2):
                    nc.gpsimd.tensor_tensor(pair_sum[:, k], tab_in[q][:, 2 * k], tab_in[q][:, 2 * k + 1],
                                            ALU.add).then_inc(pairs_added[q], 1)
                after(pool, pairs_added, s, TABLES // 2)
                nc.gpsimd.tensor_tensor(agg[q][:], pair_sum[:, 0], pair_sum[:, 1], ALU.add).then_inc(agg_ready[q], 1)

            def add_d2b(s):
                after(pool, scaled1_made, s)
                after(pool, y_made[1], s.ahead(-2))
                nc.gpsimd.tensor_tensor(hb[s.slot][:], scaled1[s.slot][:], be1_d2b[:].unsqueeze(1).to_broadcast([P, TPB, H]),
                                        ALU.add).then_inc(hb_ready[s.slot], 1)

            def third_input(s):
                q = s.slot
                after(pool, normed_ready[1], s)
                after(pool, y_made[2], s.ahead(-1))
                nc.gpsimd.tensor_tensor(scaled2[:], normed[1][q][:], G2.unsqueeze(1).to_broadcast([P, TPB, H]),
                                        ALU.mult).then_inc(scaled2_made[q], 1)
                after(pool, scaled2_made, s)
                after(pool, normed_ready[2], s.ahead(-2))
                apart(pool)
                nc.gpsimd.tensor_tensor(y[2][q][:], scaled2[:], xb[:, bass.ds(s.number() * TPB, TPB), :],
                                        ALU.add).then_inc(y_made[2][q], 1)

            pool.wait_ge(row_made, 1)
            pool.wait_ge(xb_ready, 1)
            for s in steps(pool, GROUPS, 2, TABLES_AHEAD):
                if s.ahead(NORM3).exists(GROUPS):
                    third_input(s.ahead(NORM3))
                if s.ahead(HN).exists(GROUPS):
                    add_d2b(s.ahead(HN))
                if s.ahead(TABLES_AHEAD).exists(GROUPS):
                    add_tables(s.ahead(TABLES_AHEAD))

        @block.scalar
        def _(act):
            def relu1(s):
                after(act, h1_done, s)
                after(act, h2_done, s.ahead(-2))
                nc.scalar.activation(h1[s.slot % 2][:], h1_ps[s.slot % 2][:], ACT.Relu,
                                     bias=b1_sb[:, 0:1]).then_inc(h1_ready[s.slot], 1)

            def relu2(s):
                after(act, h2_done, s)
                after(act, sum_done, s.ahead(-2))
                nc.scalar.activation(h2_hi[s.slot % 2][:], h2_ps[s.slot % 2][:], ACT.Relu).then_inc(h2_hi_ready[s.slot], 1)

            def take_sums(s):
                after(act, sum_done, s)
                for t in range(TPB):
                    after(act, scattered[t], s.ahead(-UNROLL), 16)
                nc.scalar.copy(sums[s.slot][:], sum_ps[s.slot % 2][:]).then_inc(sums_ready[s.slot], 1)

            act.wait_ge(weights_in, 16 * WEIGHTS)
            for s in steps(act, BLOCKS, UNROLL, 2):
                if s.ahead(2).exists(BLOCKS):
                    relu1(s.ahead(2))
                if s.ahead(1).exists(BLOCKS):
                    relu2(s.ahead(1))
                if s.exists(BLOCKS):
                    take_sums(s)

            act.wait_ge(counts_done, 1)
            nc.scalar.mul(count_sb[:], count_ps[:], 1.0 / SCALE).then_inc(counts_ready, 1)

            def take_agg(s):
                after(act, agg_turned, s)
                after(act, dh_done, s.ahead(-2))
                nc.scalar.copy(agg_t[s.slot][:], rows_ps[:].rearrange("p t n -> p (t n)")).then_inc(agg_t_ready[s.slot], 1)

            def take_hn(s):
                after(act, hn_turned, s)
                after(act, hid_done, s.ahead(-2), FC)
                nc.scalar.copy(hn_t[s.slot][:], sum_ps[0][:].rearrange("p t n -> p (t n)")).then_inc(hn_t_ready[s.slot], 1)

            def take_hidden(s, c):
                after(act, hid_done, s, FC, c + 1)
                after(act, ff_done, s.ahead(-2))
                nc.scalar.activation(hid[s.slot][c], h1_ps[c % 2][:], ACT.Relu,
                                     bias=d1b_sb[:, c:c + 1]).then_inc(hid_ready[s.slot], 1)

            def root(step, norms):
                for k, s in norms:
                    after(act, var_ready[k], s)
                q = step.slot
                after(act, rstd_made, step.ahead(-2))
                nc.scalar.activation(std[q][:], mean_var[q][:, :, :, 1], ACT.Sqrt, bias=eps[:, 0:1]
                                     ).then_inc(std_ready[q], 1)

            def normalize(step, k, s):
                q = step.slot
                after(act, shift_ready, step)
                after(act, [scaled1_made, scaled2_made][k] if k < 2 else stored, s.ahead(-2), 1 if k < 2 else 16)
                for t in range(TPB):
                    op = nc.scalar.activation(normed[k][s.slot][:, t, :], y[k][s.slot][:, t, :], ACT.Identity,
                                              bias=shift[q][:, k, t:t + 1], scale=rstd[q][:, k, t:t + 1])
                op.then_inc(normed_ready[k][s.slot], 1)

            act.wait_ge(eps_made, 3)
            def normalize_all(s, of=range(3)):
                for k in of:
                    if s.ahead(NORM_LEADS[k] - 1).exists(GROUPS):
                        normalize(s.ahead(NORM1 - 1), k, s.ahead(NORM_LEADS[k] - 1))

            for s in steps(act, GROUPS, 2, TURN):
                feeds = s.ahead(FEED).exists(GROUPS)
                if feeds:
                    take_hn(s.ahead(FEED))
                for k in range(3):
                    normalize_all(s, [k])
                    if feeds:
                        take_hidden(s.ahead(FEED), k)
                if feeds:
                    take_hidden(s.ahead(FEED), 3)
                if s.ahead(TURN).exists(GROUPS):
                    take_agg(s.ahead(TURN))
                norms = [(k, s.ahead(lead)) for k, lead in enumerate(NORM_LEADS) if s.ahead(lead).exists(GROUPS)]
                if norms:
                    root(s.ahead(NORM1), norms)
        @block.tensor
        def _(pe):
            pe.wait_ge(consts_made, 4)
            pe.wait_ge(weights_in, 16 * WEIGHTS)
            pe.wait_ge(pe_const, PE_CONSTS)
            nc.tensor.matmul(count_ps[:], zero_h[:], zero_h[:, 0:CPP], start=True, stop=False)

            def spread_ids(s):
                after(pe, ids_ready, s)
                after(pe, rank_made, s.ahead(-1))
                for t in range(TPB):
                    mm = nc.tensor.transpose(rows_ps[:, t, :], ids_now[s.slot][:, 0, t:t + 1].to_broadcast([P, P]), ident[:])
                mm.then_inc(rows_ready[s.slot], 1)

            def layer1(s):
                after(pe, edges_in, s, 16)
                after(pe, h1_ready, s.ahead(-2))
                for k in range(KC):
                    mm = nc.tensor.matmul(h1_ps[s.slot % 2][:], w1_sb[:, k, :], edge_in[s.slot][:, k, :],
                                          start=(k == 0), stop=(k == KC - 1))
                mm.then_inc(h1_done[s.slot], 1)

            def layer2(s):
                after(pe, h1_ready, s)
                after(pe, h2_ready, s.ahead(-2))
                h2o = h2_ps[s.slot % 2]
                nc.tensor.matmul(h2o[:], ones3[:], b2_split[:].unsqueeze(1).to_broadcast([3, TPB, H]),
                                 start=True, stop=False)
                for t in range(TPB):
                    mm = nc.tensor.matmul(h2o[:, t, :], h1[s.slot % 2][:, t * P:(t + 1) * P], w2_sb[:],
                                          start=False, stop=(t == TPB - 1))
                mm.then_inc(h2_done[s.slot], 1)

            def sum_same(s):
                after(pe, rank_made, s)
                after(pe, h2_ready, s)
                after(pe, sums_ready, s.ahead(-2))
                for t in range(TPB):
                    for part in (h2_hi, h2_lo):
                        nc.tensor.matmul(sum_ps[s.slot % 2][:, t, :], same[s.slot][:, t, :], part[s.slot % 2][:, t, :],
                                         start=(part is h2_hi), stop=(part is h2_lo))
                after(pe, rows_chosen, s)
                for t in range(TPB):
                    mm = nc.tensor.matmul(count_ps[:], hot_p[s.slot][:, t, :], hot_c[s.slot][:, t, :],
                                          start=False, stop=False)
                mm.then_inc(sum_done[s.slot], 1)

            for s in steps(pe, BLOCKS, UNROLL, 2):
                if s.ahead(2).exists(BLOCKS):
                    spread_ids(s.ahead(2))
                    layer1(s.ahead(2))
                if s.ahead(1).exists(BLOCKS):
                    layer2(s.ahead(1))
                if s.exists(BLOCKS):
                    sum_same(s)
            nc.tensor.matmul(count_ps[:], zero_h[:], zero_h[:, 0:CPP], start=False, stop=True).then_inc(counts_done, 1)

            last = Step(None, BLOCKS - 1, UNROLL)
            after(pe, rank_made, last)
            after(pe, h2_ready, last)
            after(pe, sums_ready, last)
            after(pe, sums_ready, last.ahead(-1))

            def turn_agg(s):
                after(pe, agg_ready, s)
                after(pe, agg_t_ready, s.ahead(-1))
                for t in range(TPB):
                    mm = nc.tensor.transpose(rows_ps[:, t, :], agg[s.slot][:, t, :], ident[:])
                mm.then_inc(agg_turned[s.slot], 1)

            def layer3(s):
                after(pe, agg_t_ready, s)
                after(pe, dh_x_made, s.ahead(-1))
                for t in range(TPB):
                    mm = nc.tensor.matmul(h2_ps[0][:, t, :], agg_t[s.slot][:, t * P:(t + 1) * P], w3_sb[:],
                                          start=True, stop=True)
                mm.then_inc(dh_done[s.slot], 1)

            def turn_hn(s):
                after(pe, hn_ready, s)
                after(pe, hn_t_ready, s.ahead(-1))
                for t in range(TPB):
                    mm = nc.tensor.transpose(sum_ps[0][:, t, :], hn[s.slot][:, t, :], ident[:])
                mm.then_inc(hn_turned[s.slot], 1)

            def hidden(s, c):
                if c == 0:
                    after(pe, hn_t_ready, s)
                if c < 2:
                    after(pe, hid_ready, s.ahead(-1), FC, c + 3)
                else:
                    after(pe, hid_ready, s, FC, c - 1)
                nc.tensor.matmul(h1_ps[c % 2][:], d1_sb[:, c * P:(c + 1) * P], hn_t[s.slot][:],
                                 start=True, stop=True).then_inc(hid_done[s.slot], 1)

            def project(s, t):
                if t == 0:
                    after(pe, y_made[1], s.ahead(-1))
                    after(pe, hid_ready, s, FC)
                for c in range(FC):
                    mm = nc.tensor.matmul(h2_ps[1][:, t, :], hid[s.slot][c][:, t * P:(t + 1) * P], d2_sb[:, c, :],
                                          start=(c == 0), stop=(c == FC - 1))
                if t == TPB - 1:
                    mm.then_inc(ff_done[s.slot], 1)

            for s in steps(pe, GROUPS, 2, TURN):
                if s.ahead(FEED).exists(GROUPS):
                    turn_hn(s.ahead(FEED))
                for k in range(TPB):
                    if s.ahead(FEED).exists(GROUPS):
                        hidden(s.ahead(FEED), k)
                    if s.ahead(PROJECT).exists(GROUPS):
                        project(s.ahead(PROJECT), k)
                if s.ahead(LAYER3).exists(GROUPS):
                    layer3(s.ahead(LAYER3))
                if s.ahead(TURN).exists(GROUPS):
                    turn_agg(s.ahead(TURN))

        @block.vector
        def _(dve):
            nc.vector.memset(eps[:], EPS).then_inc(eps_made, 1)
            for q in range(2):
                nc.vector.memset(mean_var[q][:], 1.0).then_inc(eps_made, 1)
            nc.vector.memset(zero_h[:], 0.0).then_inc(pe_const, 1)
            nc.vector.memset(ones3[:], 1.0).then_inc(pe_const, 1)
            done = [0]

            def then(instruction):
                done[0] += 1
                instruction.then_inc(dve_step, 1)
                dve.wait_ge(dve_step, done[0])

            def work_out_ids(a, b):
                node, part, col = (ids[:, a:b, k, :] for k in range(3))
                div = src_sb[:, a:b]
                then(nc.vector.tensor_copy(node, div))
                then(nc.vector.tensor_scalar(div, div, 2, None, ALU.logical_shift_right))
                then(nc.vector.tensor_scalar(div, div, DIV_MUL, None, ALU.mult))
                then(nc.vector.tensor_scalar(div, div, DIV_SHIFT, None, ALU.logical_shift_right))
                then(nc.vector.tensor_copy(part, div))
                then(nc.vector.scalar_tensor_tensor(out=col, in0=part, scalar=-float(CPP), in1=node,
                                                    op0=ALU.mult, op1=ALU.add))

            dve.wait_ge(src_in[0], 16)
            work_out_ids(0, FIRST_IDS)
            dve.wait_ge(consts_made, 4)
            then(nc.vector.tensor_copy(iota[:], iota_i[:]))
            then(nc.vector.tensor_copy(trash[:], trash_i[:]))
            dve.wait_ge(weights_in, 16 * WEIGHTS)
            then(nc.vector.tensor_copy(b2_part[:, 0], b2_row[:]))
            then(nc.vector.tensor_tensor(b2_rest[:, 0], b2_row[:], b2_part[:, 0], ALU.subtract))
            then(nc.vector.tensor_copy(b2_part[:, 1], b2_rest[:, 0]))
            then(nc.vector.tensor_tensor(b2_rest[:, 1], b2_rest[:, 0], b2_part[:, 1], ALU.subtract))
            then(nc.vector.tensor_copy(b2_part[:, 2], b2_rest[:, 1]))
            then(nc.vector.tensor_scalar(b2_sum[:, 0], b2_part[:, 0], ident[0:3, 0:1], None, ALU.mult))
            then(nc.vector.scalar_tensor_tensor(out=b2_sum[:, 1], in0=b2_part[:, 1], scalar=ident[0:3, 1:2],
                                                in1=b2_sum[:, 0], op0=ALU.mult, op1=ALU.add))
            nc.vector.scalar_tensor_tensor(out=b2_split[:], in0=b2_part[:, 2], scalar=ident[0:3, 2:3],
                                           in1=b2_sum[:, 1], op0=ALU.mult, op1=ALU.add).then_inc(pe_const, 1)

            def take_ids(s):
                after(dve, rows_ready, s.ahead(-UNROLL))
                after(dve, rows_chosen, s.ahead(-UNROLL))
                nc.vector.tensor_copy(ids_now[s.slot][:], ids[:, s.number()]).then_inc(ids_ready[s.slot], 1)

            def compare(s):
                k = s.slot
                after(dve, rows_ready, s)
                after(dve, ids_ready, s)
                after(dve, sum_done, s.ahead(-UNROLL))
                for t in range(TPB):
                    op = nc.vector.scalar_tensor_tensor(
                        out=same[k][:, t, :], in0=rows_ps[:, t, :], scalar=ids_now[k][:, 0, t:t + 1],
                        in1=not_before[:], op0=ALU.is_equal, op1=ALU.mult, accum_out=rank[k][:, t:t + 1])
                op.then_inc(rank_made[k], 1)

            def choose_rows(s):
                k = s.slot
                for t in range(TPB):
                    after(dve, scattered[t], s.ahead(-UNROLL), 16)
                after(dve, rank_made, s)
                nc.vector.tensor_scalar(dest_f[k][:], rank[k][:], 1.5, trash[:, 0:1],
                                        ALU.is_gt, ALU.mult).then_inc(dest_f_made[k], 1)
                after(dve, dest_f_made, s)
                nc.vector.tensor_tensor(dest[k][:], dest_f[k][:], ids_now[k][:, 0, :], ALU.max).then_inc(rows_chosen[k], 1)

            def one_hot(s):
                k = s.slot
                for t in range(TPB):
                    nc.vector.tensor_scalar(hot_p[k][:, t, :], iota[:], ids_now[k][:, 1, t:t + 1], None, ALU.is_equal)
                    nc.vector.tensor_scalar(hot_c[k][:, t, :], iota[:, 0:CPP], ids_now[k][:, 2, t:t + 1],
                                                 None, ALU.is_equal)

            def low_part(s):
                after(dve, h2_hi_ready, s)
                after(dve, sum_done, s.ahead(-2))
                nc.vector.scalar_tensor_tensor(out=h2_lo[s.slot % 2][:], in0=h2_ps[s.slot % 2][:], scalar=0.0,
                                               in1=h2_hi[s.slot % 2][:].bitcast(F32), op0=ALU.max,
                                               op1=ALU.subtract).then_inc(h2_ready[s.slot], 1)

            for s in steps(dve, BLOCKS, UNROLL, 3):
                if s.ahead(3).exists(BLOCKS):
                    take_ids(s.ahead(3))
                if s.ahead(2).exists(BLOCKS):
                    compare(s.ahead(2))
                if s.base is None and s.n == -1:
                    dve.wait_ge(src_in[1], 16)
                    work_out_ids(FIRST_IDS, BLOCKS)
                    dve.wait_ge(rows_in, 16)
                    nc.vector.tensor_tensor(be1_d2b[:], BE1, D2B, ALU.add).then_inc(row_made, 1)
                if s.ahead(1).exists(BLOCKS):
                    low_part(s.ahead(1))
                if s.ahead(2).exists(BLOCKS):
                    one_hot(s.ahead(2))
                    choose_rows(s.ahead(2))

            dve.wait_ge(x_all_in, 16)
            nc.vector.tensor_tensor(xb[:], x_sb, BE2.unsqueeze(1).to_broadcast([P, CPP, H]), ALU.add).then_inc(xb_ready, 1)

            def row_over(ap):
                return ap.unsqueeze(1).to_broadcast([P, TPB, H])

            def statistics(k, s):
                after(dve, y_made[k], s)
                after(dve, var_ready[k], s.ahead(-1))
                for t in range(TPB):
                    op = nc.vector.bn_stats(stats[k][:, t, :], y[k][s.slot][:, t, :])
                op.then_inc(stats_made[k][s.slot], 1)

            def variance(step, k, s):
                q = step.slot
                after(dve, stats_made[k], s)
                after(dve, shift_ready, step.ahead(-2))
                apart(dve)
                for t in range(TPB):
                    op = nc.vector.bn_aggr(mean_var[q][:, k, t, :], stats[k][:, t, :])
                op.then_inc(var_ready[k][s.slot], 1)

            def first_input(s):
                q, c = s.slot, s.number() * TPB
                after(dve, dh_done, s)
                after(dve, y_made[0], s.ahead(-1))
                nc.vector.tensor_copy(count_now[:], count_sb[:, bass.ds(c, TPB)])
                nc.vector.scalar_tensor_tensor(out=dh_x[:], in0=h2_ps[0][:], scalar=1.0 / SCALE,
                                               in1=x_sb[:, bass.ds(c, TPB), :], op0=ALU.mult,
                                               op1=ALU.add).then_inc(dh_x_made[q], 1)
                after(dve, dh_x_made, s)
                after(dve, normed_ready[0], s.ahead(-2))
                for t in range(TPB):
                    op = nc.vector.scalar_tensor_tensor(out=y[0][q][:, t, :], in0=B3, scalar=count_now[:, t:t + 1],
                                                        in1=dh_x[:, t, :], op0=ALU.mult, op1=ALU.add)
                op.then_inc(y_made[0][q], 1)

            def scale_first(s):
                after(dve, normed_ready[0], s)
                after(dve, hn_ready, s.ahead(-2))
                after(dve, hb_ready, s.ahead(-2))
                nc.vector.tensor_tensor(scaled1[s.slot][:], normed[0][s.slot][:], row_over(G1),
                                        ALU.mult).then_inc(scaled1_made[s.slot], 1)

            def shift_first(s):
                after(dve, scaled1_made, s)
                after(dve, hn_turned, s.ahead(-2))
                nc.vector.tensor_tensor(hn[s.slot][:], scaled1[s.slot][:], row_over(BE1),
                                        ALU.add).then_inc(hn_ready[s.slot], 1)

            def second_input(s):
                q = s.slot
                after(dve, ff_done, s)
                after(dve, hb_ready, s)
                after(dve, normed_ready[1], s.ahead(-2))
                nc.vector.tensor_tensor(y[1][q][:], h2_ps[1][:], hb[q][:], ALU.add).then_inc(y_made[1][q], 1)

            def reciprocals(step, s):
                q = step.slot
                after(dve, std_ready, step)
                for k, lead in enumerate(NORM_LEADS):
                    if s.ahead(lead - 2).exists(GROUPS):
                        after(dve, normed_ready[k], s.ahead(lead - 2))
                nc.vector.reciprocal(rstd[q][:], std[q][:]).then_inc(rstd_made[q], 1)
                after(dve, rstd_made, step)
                nc.vector.scalar_tensor_tensor(out=shift[q][:], in0=mean_var[q][:, :, :, 0], scalar=-1.0, in1=rstd[q][:],
                                               op0=ALU.mult, op1=ALU.mult).then_inc(shift_ready[q], 1)

            dve.wait_ge(counts_ready, 1)
            for s in steps(dve, GROUPS, 2, NORM1):
                step = s.ahead(NORM1)
                first, second, third, scales = (s.ahead(lead) for lead in (NORM1, NORM2, NORM3, HN))
                if first.exists(GROUPS):
                    first_input(first)
                    statistics(0, first)
                if scales.exists(GROUPS):
                    scale_first(scales)
                if first.exists(GROUPS):
                    variance(step, 0, first)
                if scales.exists(GROUPS):
                    shift_first(scales)
                if third.exists(GROUPS):
                    statistics(2, third)
                if second.exists(GROUPS):
                    second_input(second)
                if third.exists(GROUPS):
                    variance(step, 2, third)
                if second.exists(GROUPS):
                    statistics(1, second)
                    variance(step, 1, second)
                if first.exists(GROUPS) or third.exists(GROUPS):
                    reciprocals(step, s)


def kernel(x, src, dst, edge_attr_256, L0_gnn_W1_w, L0_gnn_W1_b, L0_gnn_W2_w, L0_gnn_W2_b, L0_gnn_W3_w,
           L0_gnn_W3_b, L0_gnn_ln1_g, L0_gnn_ln1_b, L0_gnn_d1_w, L0_gnn_d1_b, L0_gnn_d2_w, L0_gnn_d2_b,
           L0_gnn_ln2_g, L0_gnn_ln2_b):
    import numpy as np
    import concourse.bacc as bacc
    from concourse.bass_utils import run_bass_kernel_spmd

    def chunks(a):
        t = np.asarray(a).T
        return t.reshape(-1, P, t.shape[1]).transpose(1, 0, 2).reshape(P, -1)

    def row(a):
        return np.asarray(a).reshape(1, -1)

    def column(a, n=P):
        return np.ascontiguousarray(np.asarray(a).reshape(-1, n).T)

    edge_pad = PADDED_EDGES - EDGES
    edges = np.pad(np.asarray(edge_attr_256), ((0, edge_pad), (0, 0)))
    edges_t = np.ascontiguousarray(edges.reshape(BLOCKS, BLOCK, KC, P).transpose(0, 3, 2, 1))
    src_cols = column(np.pad(np.asarray(src), (0, edge_pad), constant_values=NODES)).reshape(P, BLOCKS, TPB)

    by_partition = {
        "w1": chunks(L0_gnn_W1_w), "b1": column(L0_gnn_W1_b), "w2": chunks(L0_gnn_W2_w),
        "w3": chunks(L0_gnn_W3_w), "d1": chunks(L0_gnn_d1_w), "d1b": column(L0_gnn_d1_b),
        "d2": chunks(L0_gnn_d2_w),
    }
    arrays = {
        "edges_t": edges_t,
        "src_cols": src_cols,
        "x": np.pad(np.asarray(x), ((0, PADDED_NODES - NODES), (0, 0))),
        "weights": np.concatenate([by_partition[name] for name in WEIGHT_COLS], axis=1),
        "rows": np.concatenate([row(a) for a in (L0_gnn_W3_b, L0_gnn_ln1_g, L0_gnn_ln1_b, L0_gnn_d2_b,
                                                 L0_gnn_ln2_g, L0_gnn_ln2_b)], axis=1),
        "b2_in": row(L0_gnn_W2_b),
    }
    nc = bacc.Bacc("TRN2", target_bir_lowering=False, num_devices=1)
    aps = {n: nc.dram_tensor(n, a.shape, mybir.dt.from_np(a.dtype), kind="ExternalInput").ap()
           for n, a in arrays.items()}
    out = nc.dram_tensor("out", (PADDED_NODES, H), F32, kind="ExternalOutput").ap()
    build(nc, out=out, **aps)
    result = run_bass_kernel_spmd(nc, [arrays], core_ids=[0])
    return result.results[0]["out"][:NODES]
```

```python
from contextlib import ExitStack

import concourse.bass as bass
from concourse import mybir

ALU = mybir.AluOpType
ACT = mybir.ActivationFunctionType
F32 = mybir.dt.float32
F32R = mybir.dt.float32r
BF16 = mybir.dt.bfloat16
I32 = mybir.dt.int32

P = 128
H = 128
K_IN = 256
KC = K_IN // P
FF = 512
FC = FF // P
NODES = 6250
EDGES = 200000
SCALE = 30.0
EPS = 1e-5

TPB = 4
BLOCK = TPB * P
SLOTS = 4
BODY = 4 * SLOTS
BLOCKS = -(-EDGES // BLOCK)
TILES = -(-EDGES // P)
PADDED_EDGES = BLOCKS * BLOCK

GROUPS = -(-NODES // (TPB * P))
CPP = GROUPS * TPB
PADDED_NODES = P * CPP
TRASH = PADDED_NODES
ZERO_ROWS = 27
RPP = -(-(CPP + 1) // ZERO_ROWS) * ZERO_ROWS
ROWS = P * RPP
DIV_SHIFT = 14
DIV_MUL = -(-(1 << DIV_SHIFT) // (CPP // 4))
assert CPP % 4 == 0 and all((n // 4 * DIV_MUL) >> DIV_SHIFT == n // CPP for n in range(PADDED_NODES))
assert PADDED_NODES // 4 * DIV_MUL < 1 << 24

FIRST_IDS = 8
TABLES = TPB
WHOLE = 2
PIECE_ROWS = 9
PACE = 1
AHEAD_OF_PIECES = 4
MARGIN = 5
FIRST_TABLES = []
for tile in range(2 * SLOTS * TPB):
    zeroed = [t for t in range(TABLES)
              if t < WHOLE or tile >= ((t + 1 - WHOLE) * -(-RPP // PIECE_ROWS) - 1) * PACE + MARGIN]
    FIRST_TABLES.append(min(zeroed, key=lambda t: max([k for k, u in enumerate(FIRST_TABLES) if u == t], default=-1)))
TABLE_ORDER = FIRST_TABLES[-TPB:]
assert sorted(TABLE_ORDER) == sorted(FIRST_TABLES[-2 * TPB:-TPB]) == list(range(TABLES))

NORM3 = 1
NORM2 = 2
PROJECT = 2
FEED = 3
HB = 3
HN = 4
NORM1 = 6
LAYER3 = 7
TURN = 8
TABLES_AHEAD = 9
FIRST_BY_VECTOR = 2
LAST_BY_VECTOR = 2
NORM_ORDER = (1, 0, 2)
NORM_LEADS = (NORM1, NORM2, NORM3)

WEIGHT_COLS = {"w1": KC * H, "b1": 1, "w2": H, "w3": H, "d1": FF, "d1b": FC, "d2": FC * H}
ROW_NAMES = ("b3", "g1", "be1", "d2b", "g2", "be2")


class Step:

    def __init__(self, base, n, slots, body=None):
        self.base, self.n, self.slots, self.body = base, n, slots, body
        self.slot = n % slots

    def ahead(self, k):
        return Step(self.base, self.n + k, self.slots, self.body)

    def number(self):
        return self.n if self.base is None else self.base * self.body + self.n

    def exists(self, count):
        return self.base is not None or 0 <= self.n < count


def steps(eng, count, slots, body, lead, whole=None):
    turns = ((count if whole is None else whole) - lead) // body
    loop = turns > 2
    for n in range(-lead, body if loop else count):
        yield Step(None, n, slots)
    if loop:
        with eng.Fori(1, turns) as turn:
            for n in range(body):
                yield Step(turn, n, slots, body)
        for n in range(turns * body, count):
            yield Step(None, n, slots)


def after(eng, sems, step, inc=1, upto=None):
    short = inc - (inc if upto is None else upto)
    value = (step.n // step.slots + 1) * inc - short
    if step.base is not None:
        by_turn = step.body // step.slots * inc
        assert by_turn + value > 0
        eng.wait_ge(sems[step.slot], step.base * by_turn + value)
    elif step.n >= 0:
        eng.wait_ge(sems[step.slot], value)


def apart(eng):
    eng.nop(nofuse=True)


def build(nc, edges_t, src_cols, x, weights, rows, b2_in, out):
    with ExitStack() as ctx:
        def sb(name, shape, dt=F32):
            return ctx.enter_context(nc.sbuf_tensor(name, shape, dt))

        def ps(name, shape):
            return ctx.enter_context(nc.psum_tensor(name, shape, F32))

        def sem(name):
            return ctx.enter_context(nc.semaphore(name))

        def sems(name, n):
            return [sem(f"{name}{k}") for k in range(n)]

        tables = [nc.dram_tensor(f"node_sums{t}", (ROWS, H), F32, kind="Internal").ap() for t in range(TABLES)]

        rows_ps = ps("rows_ps", [P, TPB, P])
        h1_ps = [ps(f"h1_ps{k}", [P, BLOCK]) for k in range(2)]
        h2_ps = [ps(f"h2_ps{k}", [P, TPB, H]) for k in range(2)]
        sum_ps = [ps(f"sum_ps{k}", [P, TPB, H]) for k in range(2)]
        count_ps = ps("count_ps", [P, CPP])

        ident = sb("ident", [P, P])
        not_before = sb("not_before", [P, P])
        iota_i = sb("iota_i", [P, P], I32)
        iota = sb("iota", [P, P], BF16)
        trash_i = sb("trash_i", [P, 1], I32)
        trash = sb("trash", [P, 1])
        ones3 = sb("ones3", [3, P], BF16)
        zero_h = sb("zero_h", [P, P], BF16)
        x_sb = sb("x_sb", [P, CPP, H])
        zeros = x_sb[:, 0:ZERO_ROWS, :]
        weights_sb = sb("weights_sb", [P, sum(WEIGHT_COLS.values())])
        at, part = 0, {}
        for name, width in WEIGHT_COLS.items():
            part[name] = weights_sb[:, at:at + width]
            at += width
        w1_sb = part["w1"].rearrange("p (k f) -> p k f", k=KC)
        w2_sb, w3_sb, d1_sb, b1_sb, d1b_sb = (part[name] for name in ("w2", "w3", "d1", "b1", "d1b"))
        d2_sb = part["d2"].rearrange("p (c f) -> p c f", c=FC)
        b2_row = sb("b2_row", [3, H])
        b2_rest = sb("b2_rest", [3, 2, H])
        b2_part = sb("b2_part", [3, 3, H], BF16)
        b2_sum = sb("b2_sum", [3, 2, H])
        b2_split = sb("b2_split", [3, H], BF16)
        bcast = sb("bcast", [P, len(ROW_NAMES), H])
        B3, G1, BE1, D2B, G2, BE2 = (bcast[:, k, :] for k in range(len(ROW_NAMES)))
        be1_d2b = sb("be1_d2b", [P, H])

        src_sb = sb("src_sb", [P, BLOCKS, TPB], I32)
        ids = sb("ids", [P, BLOCKS, 3, TPB])

        edge_in = [sb(f"edge_in{k}", [P, KC, BLOCK]) for k in range(SLOTS)]
        ids_now = [sb(f"ids_now{k}", [P, 3, TPB]) for k in range(SLOTS)]
        same = [sb(f"same{k}", [P, TPB, P], F32R) for k in range(SLOTS)]
        rank = [sb(f"rank{k}", [P, TPB]) for k in range(SLOTS)]
        dest_f = [sb(f"dest_f{k}", [P, TPB]) for k in range(SLOTS)]
        dest = [sb(f"dest{k}", [P, TPB], I32) for k in range(SLOTS)]
        hot_p = [sb(f"hot_p{k}", [P, TPB, P], BF16) for k in range(SLOTS)]
        hot_c = [sb(f"hot_c{k}", [P, TPB, CPP], BF16) for k in range(SLOTS)]
        h1 = [sb(f"h1_{k}", [P, BLOCK]) for k in range(2)]
        h2_hi = [sb(f"h2_hi{k}", [P, TPB, H], F32R) for k in range(2)]
        h2_lo = [sb(f"h2_lo{k}", [P, TPB, H], F32R) for k in range(2)]
        sums = [sb(f"sums{k}", [P, TPB, H]) for k in range(SLOTS)]

        tab_in = [sb(f"tab_in{k}", [P, TABLES, TPB, H]) for k in range(2)]
        agg, hn, hn_t = sums[0:2], sums[2:4], h1
        agg_t = [sb(f"agg_t{k}", [P, BLOCK]) for k in range(2)]
        count_sb = sb("count_sb", [P, CPP])
        xb = sb("xb", [P, CPP, H])
        dh_x = sb("dh_x", [P, TPB, H])
        count_now = sb("count_now", [P, TPB])
        y = [[sb(f"y{k}_{q}", [P, TPB, H]) for q in range(2)] for k in range(3)]
        scaled1 = [sb(f"scaled1_{k}", [P, TPB, H]) for k in range(2)]
        scaled2 = sb("scaled2", [P, TPB, H])
        hb = [sb(f"hb{k}", [P, TPB, H]) for k in range(2)]
        hid = [[edge_in[2 * k + c // KC][:, c % KC, :] for c in range(FC)] for k in range(2)]
        normed = [[sb(f"normed{k}_{q}", [P, TPB, H]) for q in range(2)] for k in range(3)]
        stats = [sb(f"stats{k}", [P, TPB, 6]) for k in range(3)]
        mean_var = [sb(f"mean_var{k}", [P, 3, TPB, 2]) for k in range(2)]
        std = [sb(f"std{k}", [P, 3, TPB]) for k in range(2)]
        rstd = [sb(f"rstd{k}", [P, 3, TPB]) for k in range(2)]
        shift = [sb(f"shift{k}", [P, 3, TPB]) for k in range(2)]
        eps = sb("eps", [P, 1])
        first_root = sb("first_root", [P, 1])

        weights_in = sem("weights_in")
        node_weights_in = sem("node_weights_in")
        src_in = sems("src_in", 2)
        consts_made = sem("consts_made")
        dve_step = sem("dve_step")
        zeros_made = sem("zeros_made")
        eps_made = sem("eps_made")
        pool_step = sem("pool_step")
        tables_zeroed = sems("tables_zeroed", TABLES)
        pe_const = sem("pe_const")
        edges_in = sems("edges_in", SLOTS)
        ids_ready = sems("ids_ready", SLOTS)
        rows_ready = sems("rows_ready", SLOTS)
        h1_done = sems("h1_done", SLOTS)
        h1_ready = sems("h1_ready", SLOTS)
        h2_done = sems("h2_done", SLOTS)
        h2_hi_ready = sems("h2_hi_ready", SLOTS)
        h2_ready = sems("h2_ready", SLOTS)
        rank_made = sems("rank_made", SLOTS)
        dest_f_made = sems("dest_f_made", SLOTS)
        rows_chosen = sems("rows_chosen", SLOTS)
        sum_done = sems("sum_done", SLOTS)
        sums_ready = sems("sums_ready", SLOTS)
        scattered = [sems(f"scattered{t}_", SLOTS) for t in range(TPB)]
        counts_done = sem("counts_done")
        counts_ready = sem("counts_ready")
        x_all_in = sem("x_all_in")
        tables_in = sems("tables_in", 2)
        pairs_added = sems("pairs_added", 2)
        agg_ready = sems("agg_ready", 2)
        agg_turned = sems("agg_turned", 2)
        agg_t_ready = sems("agg_t_ready", 2)
        dh_done = sems("dh_done", 2)
        dh_x_made = sems("dh_x_made", 2)
        y_made = [sems(f"y{k}_made", 2) for k in range(3)]
        stats_made = [sems(f"stats_made{k}_", 2) for k in range(3)]
        var_ready = [sems(f"var_ready{k}_", 2) for k in range(3)]
        std_ready = sems("std_ready", 2)
        rstd_made = sems("rstd_made", 2)
        shift_ready = sems("shift_ready", 2)
        normed_ready = [sems(f"normed_ready{k}_", 2) for k in range(3)]
        scaled1_made = sems("scaled1_made", 2)
        scaled2_made = sems("scaled2_made", 2)
        hn_ready = sems("hn_ready", 2)
        hb_ready = sems("hb_ready", 2)
        xb_ready = sem("xb_ready")
        row_made = sem("row_made")
        hn_turned = sems("hn_turned", 2)
        hn_t_ready = sems("hn_t_ready", 2)
        hid_done = sems("hid_done", 2)
        hid_ready = sems("hid_ready", 2)
        ff_done = sems("ff_done", 2)
        stored = sems("stored", 2)

        WEIGHTS = 2
        EDGE_COLS = sum(WEIGHT_COLS[name] for name in ("w1", "b1", "w2"))
        ZERO_DMAS = [RPP // (ZERO_ROWS if t < WHOLE else PIECE_ROWS) for t in range(TABLES)]
        X_GROUPS = 2
        X_DMAS = -(-GROUPS // X_GROUPS)
        PE_CONSTS = 3

        def first(s):
            return s.base is None and s.n < FIRST_BY_VECTOR

        def last(s):
            return s.base is None and s.n >= GROUPS - LAST_BY_VECTOR

        def add_tables(eng, op, s):
            q = s.slot
            after(eng, tables_in, s, 16 * TABLES)
            after(eng, agg_turned, s.ahead(-2))
            for k in range(0, TABLES, 2):
                op.tensor_tensor(tab_in[q][:, k], tab_in[q][:, k], tab_in[q][:, k + 1], ALU.add
                                 ).then_inc(pairs_added[q], 1)
            after(eng, pairs_added, s, TABLES // 2)
            op.tensor_tensor(agg[q][:], tab_in[q][:, 0], tab_in[q][:, 2], ALU.add).then_inc(agg_ready[q], 1)

        def third_input(eng, op, s):
            q = s.slot
            after(eng, normed_ready[1], s)
            after(eng, y_made[2], s.ahead(-1))
            op.tensor_tensor(scaled2[:], normed[1][q][:], G2.unsqueeze(1).to_broadcast([P, TPB, H]),
                             ALU.mult).then_inc(scaled2_made[q], 1)
            after(eng, scaled2_made, s)
            after(eng, normed_ready[2], s.ahead(-2))
            apart(eng)
            op.tensor_tensor(y[2][q][:], scaled2[:], xb[:, bass.ds(s.number() * TPB, TPB), :],
                             ALU.add).then_inc(y_made[2][q], 1)

        block = ctx.enter_context(nc.Block())

        @block.sync
        def _(sp):
            sp.dma_start(src_sb[:, 0:FIRST_IDS], src_cols[:, 0:FIRST_IDS]).then_inc(src_in[0], 16)
            sp.dma_start(weights_sb[:, 0:EDGE_COLS], weights[:, 0:EDGE_COLS]).then_inc(weights_in, 16)
            sp.dma_start(b2_row[:], b2_in.to_broadcast([3, H])).then_inc(weights_in, 16)

            def load(s):
                after(sp, h1_done, s.ahead(-SLOTS))
                sp.dma_start(edge_in[s.slot][:], edges_t[s.number()]).then_inc(edges_in[s.slot], 16)

            def zero(t, first, count):
                sp.dma_start(tables[t].rearrange("(p r) f -> p r f", p=P)[:, first:first + count],
                             zeros[:, 0:count]).then_inc(tables_zeroed[t], 16)

            load(Step(None, 0, SLOTS))
            load(Step(None, 1, SLOTS))
            sp.wait_ge(zeros_made, 2)
            for t in range(WHOLE):
                for first in range(0, RPP, ZERO_ROWS):
                    zero(t, first, ZERO_ROWS)
                if t == 0:
                    load(Step(None, 2, SLOTS))
            for n in range(3, AHEAD_OF_PIECES):
                load(Step(None, n, SLOTS))
            sp.dma_start(src_sb[:, FIRST_IDS:], src_cols[:, FIRST_IDS:]).then_inc(src_in[1], 16)
            pieces = [(t, first) for t in range(WHOLE, TABLES) for first in range(0, RPP, PIECE_ROWS)]
            loaded = AHEAD_OF_PIECES
            for k, (t, first) in enumerate(pieces):
                tile = k * PACE
                if tile % TPB == 0:
                    load(Step(None, loaded, SLOTS))
                    loaded += 1
                after(sp, scattered[tile % TPB], Step(None, tile // TPB, SLOTS), 16)
                zero(t, first, PIECE_ROWS)

            def load_node_weights():
                sp.dma_start(weights_sb[:, EDGE_COLS:], weights[:, EDGE_COLS:]).then_inc(node_weights_in, 16)
                sp.dma_start(bcast[:], rows.to_broadcast([P, len(ROW_NAMES) * H]).rearrange(
                    "p (k f) -> p k f", f=H)).then_inc(node_weights_in, 16)

            def load_x(first, count):
                first, end = first * TPB, min(first + count, GROUPS) * TPB
                sp.dma_start(x_sb[:, first:end, :], x.rearrange("(p c) f -> p c f", p=P)[:, first:end]
                             ).then_inc(x_all_in, 16)

            groups_of_x = 0
            for s in steps(sp, BLOCKS, SLOTS, BODY, SLOTS, TILES // TPB):
                if s.ahead(SLOTS).exists(BLOCKS) and (s.base is not None or s.n + SLOTS >= loaded):
                    load(s.ahead(SLOTS))
                if s.base is None and s.n > BLOCKS - 2 * SLOTS:
                    if groups_of_x == 0:
                        for t in range(TABLES):
                            sp.wait_ge(tables_zeroed[t], 16 * ZERO_DMAS[t])
                    after(sp, h1_done, s)
                    if groups_of_x == 0:
                        load_node_weights()
                    load_x(groups_of_x, X_GROUPS)
                    groups_of_x += X_GROUPS
            while groups_of_x < X_DMAS * X_GROUPS:
                load_x(groups_of_x, X_GROUPS)
                groups_of_x += X_GROUPS

            def nodes(ap, g):
                return ap.rearrange("(p g c) f -> g p c f", g=GROUPS, c=TPB)[g]

            def load_tables(s):
                after(sp, agg_ready, s.ahead(-2))
                for tile in range(TILES - TPB, TILES):
                    t = TABLE_ORDER[tile % TPB]
                    if s.base is None and s.n == 0:
                        after(sp, scattered[tile % TPB], Step(None, tile // TPB, SLOTS), 16)
                    sp.dma_start(tab_in[s.slot][:, t], nodes(tables[t][0:PADDED_NODES], s.number())
                                 ).then_inc(tables_in[s.slot], 16)

            def store(s):
                after(sp, normed_ready[2], s)
                sp.dma_start(nodes(out, s.number()), normed[2][s.slot][:]).then_inc(stored[s.slot], 16)

            for s in steps(sp, GROUPS, 2, 2, TABLES_AHEAD + 1):
                if s.ahead(TABLES_AHEAD + 1).exists(GROUPS):
                    load_tables(s.ahead(TABLES_AHEAD + 1))
                if s.exists(GROUPS):
                    store(s)
            for q in range(2):
                sp.wait_ge(stored[q], 16 * ((GROUPS + 1 - q) // 2))

        @block.gpsimd
        def _(pool):
            nc.gpsimd.memset(zeros[:, ZERO_ROWS // 2:], 0.0).then_inc(zeros_made, 1)
            nc.gpsimd.memset(ident[:], 0.0).then_inc(pool_step, 1)
            nc.gpsimd.memset(not_before[:], 1.0).then_inc(pool_step, 1)
            pool.wait_ge(pool_step, 2)
            nc.gpsimd.affine_select(out=ident[:], in_=ident[:], compare_op=ALU.not_equal, fill=1.0, base=0,
                                    pattern=[[-1, P]], channel_multiplier=1).then_inc(consts_made, 1)
            nc.gpsimd.affine_select(out=not_before[:], in_=not_before[:], compare_op=ALU.is_ge, fill=0.0, base=0,
                                    pattern=[[-1, P]], channel_multiplier=1).then_inc(consts_made, 1)
            nc.gpsimd.iota(iota_i[:], [[1, P]], base=0, channel_multiplier=0).then_inc(consts_made, 1)
            nc.gpsimd.iota(trash_i[:], [[0, 1]], base=TRASH, channel_multiplier=1).then_inc(consts_made, 1)

            def table_of(tile):
                return FIRST_TABLES[tile] if tile < len(FIRST_TABLES) else TABLE_ORDER[tile % TPB]

            def wait_for_table(tile):
                before = [i for i in range(tile) if table_of(i) == table_of(tile)]
                if before:
                    after(pool, scattered[before[-1] % TPB], Step(None, before[-1] // TPB, SLOTS), 16)
                else:
                    pool.wait_ge(tables_zeroed[table_of(tile)], 16 * ZERO_DMAS[table_of(tile)])

            def scatter(s):
                after(pool, sums_ready, s)
                after(pool, rows_chosen, s)
                for t in range(TPB if s.base is not None else min(TPB, TILES - s.n * TPB)):
                    if s.base is None:
                        wait_for_table(s.n * TPB + t)
                    else:
                        after(pool, scattered[t], s.ahead(-1), 16)
                    table = tables[TABLE_ORDER[t] if s.base is not None else table_of(s.n * TPB + t)]
                    apart(pool)
                    pool.indirect_dma_start(
                        table, bass.IndirectOffsetOnAxis(ap=dest[s.slot][:, t:t + 1], axis=0),
                        sums[s.slot][:, t, :], None, compute_op=ALU.add).then_inc(scattered[t][s.slot], 16)

            for s in steps(pool, BLOCKS, SLOTS, BODY, SLOTS, TILES // TPB):
                if s.ahead(SLOTS).exists(BLOCKS):
                    scatter(s.ahead(SLOTS))

            def add_d2b(s):
                after(pool, scaled1_made, s)
                after(pool, y_made[1], s.ahead(-2))
                nc.gpsimd.tensor_tensor(hb[s.slot][:], scaled1[s.slot][:], be1_d2b[:].unsqueeze(1).to_broadcast([P, TPB, H]),
                                        ALU.add).then_inc(hb_ready[s.slot], 1)

            pool.wait_ge(row_made, 1)
            pool.wait_ge(xb_ready, 1)
            for s in steps(pool, GROUPS, 2, 2, TABLES_AHEAD):
                if s.ahead(NORM3).exists(GROUPS) and not last(s.ahead(NORM3)):
                    third_input(pool, nc.gpsimd, s.ahead(NORM3))
                if s.ahead(HB).exists(GROUPS):
                    add_d2b(s.ahead(HB))
                if s.ahead(TABLES_AHEAD).exists(GROUPS) and not first(s.ahead(TABLES_AHEAD)):
                    add_tables(pool, nc.gpsimd, s.ahead(TABLES_AHEAD))

        @block.scalar
        def _(act):
            def relu1(s):
                after(act, h1_done, s)
                after(act, h2_done, s.ahead(-2))
                nc.scalar.activation(h1[s.slot % 2][:], h1_ps[s.slot % 2][:], ACT.Relu,
                                     bias=b1_sb[:, 0:1]).then_inc(h1_ready[s.slot], 1)

            def relu2(s):
                after(act, h2_done, s)
                after(act, sum_done, s.ahead(-2))
                nc.scalar.activation(h2_hi[s.slot % 2][:], h2_ps[s.slot % 2][:], ACT.Relu).then_inc(h2_hi_ready[s.slot], 1)

            def take_sums(s):
                after(act, sum_done, s)
                for t in range(TPB):
                    after(act, scattered[t], s.ahead(-SLOTS), 16)
                nc.scalar.copy(sums[s.slot][:], sum_ps[s.slot % 2][:]).then_inc(sums_ready[s.slot], 1)

            act.wait_ge(eps_made, 3)
            nc.scalar.activation(first_root[:], eps[:], ACT.Sqrt)
            act.wait_ge(weights_in, 16 * WEIGHTS)
            for s in steps(act, BLOCKS, SLOTS, BODY, 2, TILES // TPB):
                if s.ahead(2).exists(BLOCKS):
                    relu1(s.ahead(2))
                if s.ahead(1).exists(BLOCKS):
                    relu2(s.ahead(1))
                if s.exists(BLOCKS):
                    take_sums(s)

            act.wait_ge(node_weights_in, 32)
            act.wait_ge(counts_done, 1)
            nc.scalar.mul(count_sb[:], count_ps[:], 1.0 / SCALE).then_inc(counts_ready, 1)

            def take_agg(s):
                after(act, agg_turned, s)
                after(act, dh_done, s.ahead(-2))
                nc.scalar.copy(agg_t[s.slot][:], rows_ps[:].rearrange("p t n -> p (t n)")).then_inc(agg_t_ready[s.slot], 1)

            def take_hn(s):
                after(act, hn_turned, s)
                after(act, hid_done, s.ahead(-2), FC)
                nc.scalar.copy(hn_t[s.slot][:], sum_ps[0][:].rearrange("p t n -> p (t n)")).then_inc(hn_t_ready[s.slot], 1)

            def take_hidden(s, c):
                after(act, hid_done, s, FC, c + 1)
                after(act, ff_done, s.ahead(-2))
                nc.scalar.activation(hid[s.slot][c], h1_ps[c % 2][:], ACT.Relu,
                                     bias=d1b_sb[:, c:c + 1]).then_inc(hid_ready[s.slot], 1)

            def root(step, norms):
                for k, s in norms:
                    after(act, var_ready[k], s)
                q = step.slot
                after(act, rstd_made, step.ahead(-2))
                nc.scalar.activation(std[q][:], mean_var[q][:, :, :, 1], ACT.Sqrt, bias=eps[:, 0:1]
                                     ).then_inc(std_ready[q], 1)

            def normalize(step, k, s):
                q = step.slot
                after(act, shift_ready, step)
                after(act, [scaled1_made, scaled2_made][k] if k < 2 else stored, s.ahead(-2), 1 if k < 2 else 16)
                for t in range(TPB):
                    op = nc.scalar.activation(normed[k][s.slot][:, t, :], y[k][s.slot][:, t, :], ACT.Identity,
                                              bias=shift[q][:, k, t:t + 1], scale=rstd[q][:, k, t:t + 1])
                op.then_inc(normed_ready[k][s.slot], 1)

            def normalize_all(s, of):
                for k in of:
                    if s.ahead(NORM_LEADS[k] - 1).exists(GROUPS):
                        normalize(s.ahead(NORM1 - 1), k, s.ahead(NORM_LEADS[k] - 1))

            for s in steps(act, GROUPS, 2, 2, TURN):
                feeds = s.ahead(FEED).exists(GROUPS)
                for c in range(FC):
                    if feeds:
                        take_hidden(s.ahead(FEED), c)
                    if c < len(NORM_ORDER):
                        normalize_all(s, [NORM_ORDER[c]])
                if s.ahead(HN).exists(GROUPS):
                    take_hn(s.ahead(HN))
                filling = s.base is None and s.n < -FEED
                if s.ahead(TURN).exists(GROUPS) and not filling:
                    take_agg(s.ahead(TURN))
                norms = [(k, s.ahead(lead)) for k, lead in enumerate(NORM_LEADS) if s.ahead(lead).exists(GROUPS)]
                if norms:
                    root(s.ahead(NORM1), norms)
                if s.ahead(TURN).exists(GROUPS) and filling:
                    take_agg(s.ahead(TURN))

        @block.tensor
        def _(pe):
            pe.wait_ge(consts_made, 4)
            pe.wait_ge(weights_in, 16 * WEIGHTS)
            pe.wait_ge(pe_const, PE_CONSTS)
            nc.tensor.matmul(count_ps[:], zero_h[:], zero_h[:, 0:CPP], start=True, stop=False)

            def spread_ids(s):
                after(pe, ids_ready, s)
                after(pe, rank_made, s.ahead(-1))
                for t in range(TPB):
                    mm = nc.tensor.transpose(rows_ps[:, t, :], ids_now[s.slot][:, 0, t:t + 1].to_broadcast([P, P]), ident[:])
                mm.then_inc(rows_ready[s.slot], 1)

            def layer1(s):
                after(pe, edges_in, s, 16)
                after(pe, h1_ready, s.ahead(-2))
                for k in range(KC):
                    mm = nc.tensor.matmul(h1_ps[s.slot % 2][:], w1_sb[:, k, :], edge_in[s.slot][:, k, :],
                                          start=(k == 0), stop=(k == KC - 1))
                mm.then_inc(h1_done[s.slot], 1)

            def layer2(s):
                after(pe, h1_ready, s)
                after(pe, h2_ready, s.ahead(-2))
                h2o = h2_ps[s.slot % 2]
                nc.tensor.matmul(h2o[:], ones3[:], b2_split[:].unsqueeze(1).to_broadcast([3, TPB, H]),
                                 start=True, stop=False)
                for t in range(TPB):
                    mm = nc.tensor.matmul(h2o[:, t, :], h1[s.slot % 2][:, t * P:(t + 1) * P], w2_sb[:],
                                          start=False, stop=(t == TPB - 1))
                mm.then_inc(h2_done[s.slot], 1)

            def sum_same(s):
                after(pe, rank_made, s)
                after(pe, h2_ready, s)
                after(pe, sums_ready, s.ahead(-2))
                for t in range(TPB):
                    for part in (h2_hi, h2_lo):
                        nc.tensor.matmul(sum_ps[s.slot % 2][:, t, :], same[s.slot][:, t, :], part[s.slot % 2][:, t, :],
                                         start=(part is h2_hi), stop=(part is h2_lo))
                after(pe, rows_chosen, s)
                for t in range(TPB):
                    mm = nc.tensor.matmul(count_ps[:], hot_p[s.slot][:, t, :], hot_c[s.slot][:, t, :],
                                          start=False, stop=False)
                mm.then_inc(sum_done[s.slot], 1)

            for s in steps(pe, BLOCKS, SLOTS, BODY, 2, TILES // TPB):
                if s.ahead(2).exists(BLOCKS):
                    spread_ids(s.ahead(2))
                    layer1(s.ahead(2))
                if s.ahead(1).exists(BLOCKS):
                    layer2(s.ahead(1))
                if s.exists(BLOCKS):
                    sum_same(s)
            nc.tensor.matmul(count_ps[:], zero_h[:], zero_h[:, 0:CPP], start=False, stop=True).then_inc(counts_done, 1)

            final = Step(None, BLOCKS - 1, SLOTS)
            pe.wait_ge(node_weights_in, 32)
            after(pe, rank_made, final)
            after(pe, h2_ready, final)
            after(pe, sums_ready, final)
            after(pe, sums_ready, final.ahead(-1))

            def turn_agg(s):
                after(pe, agg_ready, s)
                after(pe, agg_t_ready, s.ahead(-1))
                for t in range(TPB):
                    mm = nc.tensor.transpose(rows_ps[:, t, :], agg[s.slot][:, t, :], ident[:])
                mm.then_inc(agg_turned[s.slot], 1)

            def layer3(s):
                after(pe, agg_t_ready, s)
                after(pe, dh_x_made, s.ahead(-1))
                for t in range(TPB):
                    mm = nc.tensor.matmul(h2_ps[0][:, t, :], agg_t[s.slot][:, t * P:(t + 1) * P], w3_sb[:],
                                          start=True, stop=True)
                mm.then_inc(dh_done[s.slot], 1)

            def turn_hn(s):
                after(pe, hn_ready, s)
                after(pe, hn_t_ready, s.ahead(-1))
                for t in range(TPB):
                    mm = nc.tensor.transpose(sum_ps[0][:, t, :], hn[s.slot][:, t, :], ident[:])
                mm.then_inc(hn_turned[s.slot], 1)

            def hidden(s, c):
                if c == 0:
                    after(pe, hn_t_ready, s)
                if c < 2:
                    after(pe, hid_ready, s.ahead(-1), FC, c + 3)
                else:
                    after(pe, hid_ready, s, FC, c - 1)
                nc.tensor.matmul(h1_ps[c % 2][:], d1_sb[:, c * P:(c + 1) * P], hn_t[s.slot][:],
                                 start=True, stop=True).then_inc(hid_done[s.slot], 1)

            def project(s, t):
                if t == 0:
                    after(pe, y_made[1], s.ahead(-1))
                    after(pe, hid_ready, s, FC)
                for c in range(FC):
                    mm = nc.tensor.matmul(h2_ps[1][:, t, :], hid[s.slot][c][:, t * P:(t + 1) * P], d2_sb[:, c, :],
                                          start=(c == 0), stop=(c == FC - 1))
                if t == TPB - 1:
                    mm.then_inc(ff_done[s.slot], 1)

            for s in steps(pe, GROUPS, 2, 2, TURN):
                for k in range(TPB):
                    if s.ahead(FEED).exists(GROUPS):
                        hidden(s.ahead(FEED), k)
                    if s.ahead(PROJECT).exists(GROUPS):
                        project(s.ahead(PROJECT), k)
                if s.ahead(HN).exists(GROUPS):
                    turn_hn(s.ahead(HN))
                if s.ahead(LAYER3).exists(GROUPS):
                    layer3(s.ahead(LAYER3))
                if s.ahead(TURN).exists(GROUPS):
                    turn_agg(s.ahead(TURN))

        @block.vector
        def _(dve):
            nc.vector.memset(eps[:], EPS).then_inc(eps_made, 1)
            for q in range(2):
                nc.vector.memset(mean_var[q][:], 1.0).then_inc(eps_made, 1)
            half = ZERO_ROWS // 2
            nc.vector.memset(zeros[:, 0:half], 0.0).then_inc(zeros_made, 1)
            nc.vector.memset(zero_h[:], 0.0).then_inc(pe_const, 1)
            nc.vector.memset(ones3[:], 1.0).then_inc(pe_const, 1)
            done = [0]

            def then(instruction):
                done[0] += 1
                instruction.then_inc(dve_step, 1)
                dve.wait_ge(dve_step, done[0])

            def work_out_ids(a, b):
                node, part, col = (ids[:, a:b, k, :] for k in range(3))
                div = src_sb[:, a:b]
                then(nc.vector.tensor_copy(node, div))
                then(nc.vector.tensor_scalar(div, div, 2, None, ALU.logical_shift_right))
                then(nc.vector.tensor_scalar(div, div, DIV_MUL, None, ALU.mult))
                then(nc.vector.tensor_scalar(div, div, DIV_SHIFT, None, ALU.logical_shift_right))
                then(nc.vector.tensor_copy(part, div))
                then(nc.vector.scalar_tensor_tensor(out=col, in0=part, scalar=-float(CPP), in1=node,
                                                    op0=ALU.mult, op1=ALU.add))

            dve.wait_ge(src_in[0], 16)
            work_out_ids(0, FIRST_IDS)
            dve.wait_ge(consts_made, 4)
            then(nc.vector.tensor_copy(iota[:], iota_i[:]))
            then(nc.vector.tensor_copy(trash[:], trash_i[:]))
            dve.wait_ge(weights_in, 16 * WEIGHTS)
            then(nc.vector.tensor_copy(b2_part[:, 0], b2_row[:]))
            then(nc.vector.tensor_tensor(b2_rest[:, 0], b2_row[:], b2_part[:, 0], ALU.subtract))
            then(nc.vector.tensor_copy(b2_part[:, 1], b2_rest[:, 0]))
            then(nc.vector.tensor_tensor(b2_rest[:, 1], b2_rest[:, 0], b2_part[:, 1], ALU.subtract))
            then(nc.vector.tensor_copy(b2_part[:, 2], b2_rest[:, 1]))
            then(nc.vector.tensor_scalar(b2_sum[:, 0], b2_part[:, 0], ident[0:3, 0:1], None, ALU.mult))
            then(nc.vector.scalar_tensor_tensor(out=b2_sum[:, 1], in0=b2_part[:, 1], scalar=ident[0:3, 1:2],
                                                in1=b2_sum[:, 0], op0=ALU.mult, op1=ALU.add))
            nc.vector.scalar_tensor_tensor(out=b2_split[:], in0=b2_part[:, 2], scalar=ident[0:3, 2:3],
                                           in1=b2_sum[:, 1], op0=ALU.mult, op1=ALU.add).then_inc(pe_const, 1)

            def take_ids(s):
                after(dve, rows_ready, s.ahead(-SLOTS))
                after(dve, rows_chosen, s.ahead(-SLOTS))
                nc.vector.tensor_copy(ids_now[s.slot][:], ids[:, s.number()]).then_inc(ids_ready[s.slot], 1)

            def compare(s):
                k = s.slot
                after(dve, rows_ready, s)
                after(dve, ids_ready, s)
                after(dve, sum_done, s.ahead(-SLOTS))
                for t in range(TPB):
                    op = nc.vector.scalar_tensor_tensor(
                        out=same[k][:, t, :], in0=rows_ps[:, t, :], scalar=ids_now[k][:, 0, t:t + 1],
                        in1=not_before[:], op0=ALU.is_equal, op1=ALU.mult, accum_out=rank[k][:, t:t + 1])
                op.then_inc(rank_made[k], 1)

            def choose_rows(s):
                k = s.slot
                for t in range(TPB):
                    after(dve, scattered[t], s.ahead(-SLOTS), 16)
                after(dve, rank_made, s)
                nc.vector.tensor_scalar(dest_f[k][:], rank[k][:], 1.5, trash[:, 0:1],
                                        ALU.is_gt, ALU.mult).then_inc(dest_f_made[k], 1)
                after(dve, dest_f_made, s)
                nc.vector.tensor_tensor(dest[k][:], dest_f[k][:], ids_now[k][:, 0, :], ALU.max).then_inc(rows_chosen[k], 1)

            def one_hot(s):
                k = s.slot
                for t in range(TPB):
                    nc.vector.tensor_scalar(hot_p[k][:, t, :], iota[:], ids_now[k][:, 1, t:t + 1], None, ALU.is_equal)
                    nc.vector.tensor_scalar(hot_c[k][:, t, :], iota[:, 0:CPP], ids_now[k][:, 2, t:t + 1],
                                                 None, ALU.is_equal)

            def low_part(s):
                after(dve, h2_hi_ready, s)
                after(dve, sum_done, s.ahead(-2))
                nc.vector.scalar_tensor_tensor(out=h2_lo[s.slot % 2][:], in0=h2_ps[s.slot % 2][:], scalar=0.0,
                                               in1=h2_hi[s.slot % 2][:].bitcast(F32), op0=ALU.max,
                                               op1=ALU.subtract).then_inc(h2_ready[s.slot], 1)

            for s in steps(dve, BLOCKS, SLOTS, BODY, 3, TILES // TPB):
                if s.ahead(3).exists(BLOCKS):
                    take_ids(s.ahead(3))
                if s.ahead(2).exists(BLOCKS):
                    compare(s.ahead(2))
                if s.base is None and s.n == SLOTS - 1:
                    dve.wait_ge(src_in[1], 16)
                    work_out_ids(FIRST_IDS, BLOCKS)
                if s.ahead(1).exists(BLOCKS):
                    low_part(s.ahead(1))
                if s.ahead(2).exists(BLOCKS):
                    one_hot(s.ahead(2))
                    choose_rows(s.ahead(2))

            dve.wait_ge(node_weights_in, 32)
            nc.vector.tensor_tensor(be1_d2b[:], BE1, D2B, ALU.add).then_inc(row_made, 1)
            dve.wait_ge(x_all_in, 16 * X_DMAS)
            nc.vector.tensor_tensor(xb[:], x_sb[:], BE2.unsqueeze(1).to_broadcast([P, CPP, H]), ALU.add).then_inc(xb_ready, 1)

            def row_over(ap):
                return ap.unsqueeze(1).to_broadcast([P, TPB, H])

            def statistics(k, s):
                after(dve, y_made[k], s)
                after(dve, var_ready[k], s.ahead(-1))
                for t in range(TPB):
                    op = nc.vector.bn_stats(stats[k][:, t, :], y[k][s.slot][:, t, :])
                op.then_inc(stats_made[k][s.slot], 1)

            def variance(step, k, s):
                q = step.slot
                after(dve, stats_made[k], s)
                after(dve, shift_ready, step.ahead(-2))
                apart(dve)
                for t in range(TPB):
                    op = nc.vector.bn_aggr(mean_var[q][:, k, t, :], stats[k][:, t, :])
                op.then_inc(var_ready[k][s.slot], 1)

            def first_input(s):
                q, c = s.slot, s.number() * TPB
                after(dve, dh_done, s)
                after(dve, y_made[0], s.ahead(-1))
                nc.vector.tensor_copy(count_now[:], count_sb[:, bass.ds(c, TPB)])
                nc.vector.scalar_tensor_tensor(out=dh_x[:], in0=h2_ps[0][:], scalar=1.0 / SCALE,
                                               in1=x_sb[:, bass.ds(c, TPB), :], op0=ALU.mult,
                                               op1=ALU.add).then_inc(dh_x_made[q], 1)
                after(dve, dh_x_made, s)
                after(dve, normed_ready[0], s.ahead(-2))
                for t in range(TPB):
                    op = nc.vector.scalar_tensor_tensor(out=y[0][q][:, t, :], in0=B3, scalar=count_now[:, t:t + 1],
                                                        in1=dh_x[:, t, :], op0=ALU.mult, op1=ALU.add)
                op.then_inc(y_made[0][q], 1)

            def scale_first(s):
                after(dve, normed_ready[0], s)
                after(dve, hn_ready, s.ahead(-2))
                after(dve, hb_ready, s.ahead(-2))
                nc.vector.tensor_tensor(scaled1[s.slot][:], normed[0][s.slot][:], row_over(G1),
                                        ALU.mult).then_inc(scaled1_made[s.slot], 1)

            def shift_first(s):
                after(dve, scaled1_made, s)
                after(dve, hn_turned, s.ahead(-2))
                nc.vector.tensor_tensor(hn[s.slot][:], scaled1[s.slot][:], row_over(BE1),
                                        ALU.add).then_inc(hn_ready[s.slot], 1)

            def second_input(s):
                q = s.slot
                after(dve, ff_done, s)
                after(dve, hb_ready, s)
                after(dve, normed_ready[1], s.ahead(-2))
                nc.vector.tensor_tensor(y[1][q][:], h2_ps[1][:], hb[q][:], ALU.add).then_inc(y_made[1][q], 1)

            def reciprocals(step, s):
                q = step.slot
                after(dve, std_ready, step)
                for k, lead in enumerate(NORM_LEADS):
                    if s.ahead(lead - 2).exists(GROUPS):
                        after(dve, normed_ready[k], s.ahead(lead - 2))
                nc.vector.reciprocal(rstd[q][:], std[q][:]).then_inc(rstd_made[q], 1)
                after(dve, rstd_made, step)
                nc.vector.scalar_tensor_tensor(out=shift[q][:], in0=mean_var[q][:, :, :, 0], scalar=-1.0, in1=rstd[q][:],
                                               op0=ALU.mult, op1=ALU.mult).then_inc(shift_ready[q], 1)

            dve.wait_ge(counts_ready, 1)
            for n in range(FIRST_BY_VECTOR):
                add_tables(dve, nc.vector, Step(None, n, 2))
            for s in steps(dve, GROUPS, 2, 2, NORM1):
                step = s.ahead(NORM1)
                n1, n2, n3, scales = (s.ahead(lead) for lead in (NORM1, NORM2, NORM3, HN))
                if scales.exists(GROUPS):
                    shift_first(scales)
                if n1.exists(GROUPS):
                    first_input(n1)
                    statistics(0, n1)
                    variance(step, 0, n1)
                if n3.exists(GROUPS) and last(n3):
                    if n2.exists(GROUPS):
                        second_input(n2)
                        statistics(1, n2)
                        variance(step, 1, n2)
                    third_input(dve, nc.vector, n3)
                    statistics(2, n3)
                    variance(step, 2, n3)
                else:
                    if n3.exists(GROUPS):
                        statistics(2, n3)
                    if n2.exists(GROUPS):
                        second_input(n2)
                    if n3.exists(GROUPS):
                        variance(step, 2, n3)
                    if n2.exists(GROUPS):
                        statistics(1, n2)
                        variance(step, 1, n2)
                if scales.ahead(1).exists(GROUPS):
                    scale_first(scales.ahead(1))
                if n1.exists(GROUPS) or n3.exists(GROUPS):
                    reciprocals(step, s)


def kernel(x, src, dst, edge_attr_256, L0_gnn_W1_w, L0_gnn_W1_b, L0_gnn_W2_w, L0_gnn_W2_b, L0_gnn_W3_w,
           L0_gnn_W3_b, L0_gnn_ln1_g, L0_gnn_ln1_b, L0_gnn_d1_w, L0_gnn_d1_b, L0_gnn_d2_w, L0_gnn_d2_b,
           L0_gnn_ln2_g, L0_gnn_ln2_b):
    import numpy as np
    import concourse.bacc as bacc
    from concourse.bass_utils import run_bass_kernel_spmd

    def chunks(a):
        t = np.asarray(a).T
        return t.reshape(-1, P, t.shape[1]).transpose(1, 0, 2).reshape(P, -1)

    def row(a):
        return np.asarray(a).reshape(1, -1)

    def column(a, n=P):
        return np.ascontiguousarray(np.asarray(a).reshape(-1, n).T)

    edge_pad = PADDED_EDGES - EDGES
    edges = np.pad(np.asarray(edge_attr_256), ((0, edge_pad), (0, 0)))
    edges_t = np.ascontiguousarray(edges.reshape(BLOCKS, BLOCK, KC, P).transpose(0, 3, 2, 1))
    src_cols = column(np.pad(np.asarray(src), (0, edge_pad), constant_values=NODES)).reshape(P, BLOCKS, TPB)

    by_partition = {
        "w1": chunks(L0_gnn_W1_w), "b1": column(L0_gnn_W1_b), "w2": chunks(L0_gnn_W2_w),
        "w3": chunks(L0_gnn_W3_w), "d1": chunks(L0_gnn_d1_w), "d1b": column(L0_gnn_d1_b),
        "d2": chunks(L0_gnn_d2_w),
    }
    arrays = {
        "edges_t": edges_t,
        "src_cols": src_cols,
        "x": np.pad(np.asarray(x), ((0, PADDED_NODES - NODES), (0, 0))),
        "weights": np.concatenate([by_partition[name] for name in WEIGHT_COLS], axis=1),
        "rows": np.concatenate([row(a) for a in (L0_gnn_W3_b, L0_gnn_ln1_g, L0_gnn_ln1_b, L0_gnn_d2_b,
                                                 L0_gnn_ln2_g, L0_gnn_ln2_b)], axis=1),
        "b2_in": row(L0_gnn_W2_b),
    }
    nc = bacc.Bacc("TRN2", target_bir_lowering=False, num_devices=1)
    aps = {n: nc.dram_tensor(n, a.shape, mybir.dt.from_np(a.dtype), kind="ExternalInput").ap()
           for n, a in arrays.items()}
    out = nc.dram_tensor("out", (PADDED_NODES, H), F32, kind="ExternalOutput").ap()
    build(nc, out=out, **aps)
    result = run_bass_kernel_spmd(nc, [arrays], core_ids=[0])
    return result.results[0]["out"][:NODES]
```
